# Optimizing a Trainium2 kernel written in Bass

```python
import numpy as np
import jax
import jax.numpy as jnp

def _softmax(x, axis=-1):
    return jax.nn.softmax(x, axis=axis)

def _gelu(x):
    return jax.nn.gelu(x, approximate=True)

def _silu(x):
    return jax.nn.silu(x)

def _sigmoid(x):
    return jax.nn.sigmoid(x)

def _layernorm(x, axis=-1, eps=1e-05):
    m = jnp.mean(x, axis=axis, keepdims=True)
    v = jnp.var(x, axis=axis, keepdims=True)
    return (x - m) / jnp.sqrt(v + eps)

def _scatter_add(tgt, idx, src, axis=0):
    return tgt.at[idx].add(src)

def _segment_sum(src, seg, n):
    return jax.ops.segment_sum(src, seg, n)
kernel_name = 'mk_gnn_preln_d2_gnn_r8_0fe3b5'

def setup_inputs(seed: int=0):
    np.random.seed(seed)
    _w = jnp.asarray

    def _rec_inputs():
        import jax
        import jax.numpy as jnp
        _gk = jax.random.key(seed)
        x = -0.0005121 + 1.001 * jax.random.normal(jax.random.fold_in(_gk, 1), (6250, 64), jnp.float32)
        src = jax.random.randint(jax.random.fold_in(_gk, 2), (200000,), 0, 6250, jnp.int32)
        dst = jnp.minimum((6250 * jax.random.uniform(jax.random.fold_in(_gk, 3), (200000,)) ** 2.0).astype(jnp.int32), 49999)
        _o = jnp.argsort(dst, stable=True)
        src = src[_o]
        dst = dst[_o]
        edge_attr_64 = -2.25437e-05 + 0.999858 * jax.random.normal(jax.random.fold_in(_gk, 12), (200000, 64), jnp.float32)
        edge_weight = jax.random.uniform(jax.random.fold_in(_gk, 13), (200000,), jnp.float32, 0.0, 1)
        return (x, src, dst, edge_attr_64, edge_weight)
    x, src, dst, edge_attr_64, edge_weight = _rec_inputs()

    def _L0_gnn_setup():
        import jax, jax.numpy as jnp
        import numpy as np
        N_NODES = 6250
        N_EDGES = 100000
        D_IN = 64
        D_OUT = 64
        key = jax.random.key(seed)
        k_x, k_src, k_dst, k_w, k_b = jax.random.split(key, 5)
        x = jax.random.normal(k_x, (N_NODES, D_IN), dtype=jnp.float32)
        edge_src = jax.random.randint(k_src, (N_EDGES,), 0, N_NODES, dtype=jnp.int64)
        edge_dst = jax.random.randint(k_dst, (N_EDGES,), 0, N_NODES, dtype=jnp.int64)
        edge_w = jnp.ones((N_EDGES,), dtype=jnp.float32)
        W = jax.random.normal(k_w, (D_IN, D_OUT), dtype=jnp.float32) * (1.0 / np.sqrt(D_IN))
        b = jax.random.normal(k_b, (D_OUT,), dtype=jnp.float32) * 0.01
        return {'x': x, 'edge_src': edge_src, 'edge_dst': edge_dst, 'edge_w': edge_w, 'W': W, 'b': b}
    _L0_gnn_all = _L0_gnn_setup()
    _L0_gnn_in = {k: v for k, v in _L0_gnn_all.items() if k in ('W', 'b')}
    del _L0_gnn_all

    def _L1_gnn_setup():
        import jax, jax.numpy as jnp
        import numpy as np
        N_NODES = 12500
        N_EDGES = 125000
        D_NODE = 64
        D_EDGE = 64
        key = jax.random.key(seed)
        ks = jax.random.split(key, 8)
        node_features = jax.random.normal(ks[0], (N_NODES, D_NODE), dtype=jnp.float32)
        edge_features = jax.random.normal(ks[1], (N_EDGES, D_EDGE), dtype=jnp.float32)
        src = jax.random.randint(ks[2], (N_EDGES,), 0, N_NODES)
        tgt = jax.random.randint(ks[3], (N_EDGES,), 0, N_NODES)
        fan_msg = D_NODE + D_EDGE
        W_msg = jax.random.uniform(ks[4], (fan_msg, D_NODE), dtype=jnp.float32, minval=-1.0 / np.sqrt(fan_msg), maxval=1.0 / np.sqrt(fan_msg))
        b_msg = jnp.zeros((D_NODE,), dtype=jnp.float32)
        W_upd = jax.random.uniform(ks[5], (D_NODE, D_NODE), dtype=jnp.float32, minval=-1.0 / np.sqrt(D_NODE), maxval=1.0 / np.sqrt(D_NODE))
        b_upd = jnp.zeros((D_NODE,), dtype=jnp.float32)
        eps = jnp.zeros((1,), dtype=jnp.float32)
        return {'node_features': node_features, 'edge_features': edge_features, 'W_msg': W_msg, 'b_msg': b_msg, 'W_upd': W_upd, 'b_upd': b_upd, 'eps': eps, 'src': src, 'tgt': tgt}
    _L1_gnn_all = _L1_gnn_setup()
    _L1_gnn_in = {k: v for k, v in _L1_gnn_all.items() if k in ('W_msg', 'b_msg', 'W_upd', 'b_upd', 'eps')}
    del _L1_gnn_all
    return {'x': x, 'src': src, 'dst': dst, 'edge_attr_64': edge_attr_64, 'edge_weight': edge_weight, 'L0_gnn_W': _L0_gnn_in['W'], 'L0_gnn_b': _L0_gnn_in['b'], 'L1_gnn_W_msg': _L1_gnn_in['W_msg'], 'L1_gnn_b_msg': _L1_gnn_in['b_msg'], 'L1_gnn_W_upd': _L1_gnn_in['W_upd'], 'L1_gnn_b_upd': _L1_gnn_in['b_upd'], 'L1_gnn_eps': _L1_gnn_in['eps']}

def reference(x, src, dst, edge_attr_64, edge_weight, L0_gnn_W, L0_gnn_b, L1_gnn_W_msg, L1_gnn_b_msg, L1_gnn_W_upd, L1_gnn_b_upd, L1_gnn_eps):
    import jax
    import jax.numpy as jnp

    def _L0_gnn_ref(x, edge_src, edge_dst, edge_w, W, b):
        import jax, jax.numpy as jnp
        import numpy as np
        N_NODES = 6250
        N_EDGES = 100000
        D_IN = 64
        D_OUT = 64
        h = x @ W + b
        msgs = edge_w[:, None] * h[edge_src]
        agg = jax.ops.segment_sum(msgs, edge_dst, num_segments=N_NODES)
        deg = jax.ops.segment_sum(edge_w, edge_dst, num_segments=N_NODES)
        agg = agg / (deg[:, None] + 1e-06)
        return jax.nn.relu(agg)

    def _L1_gnn_ref(node_features, edge_features, W_msg, b_msg, W_upd, b_upd, eps, src, tgt):
        import jax, jax.numpy as jnp
        import numpy as np
        N_NODES = 12500
        N_EDGES = 125000
        D_NODE = 64
        D_EDGE = 64
        src_feats = node_features[src]
        msg_in = jnp.concatenate([src_feats, edge_features], axis=-1)
        messages = jax.nn.gelu(msg_in @ W_msg + b_msg)
        agg = jax.ops.segment_sum(messages, tgt, num_segments=node_features.shape[0])
        h = (1.0 + eps) * node_features + agg
        out = jax.nn.gelu(h @ W_upd + b_upd)
        return out
    h = jnp.maximum(_layernorm(x, axis=-1), 0.0)
    x = x + _L0_gnn_ref(h, src, dst, edge_weight, L0_gnn_W, L0_gnn_b)
    h = jnp.maximum(_layernorm(x, axis=-1), 0.0)
    x = x + _L1_gnn_ref(h, edge_attr_64, L1_gnn_W_msg, L1_gnn_b_msg, L1_gnn_W_upd, L1_gnn_b_upd, L1_gnn_eps, src, dst)
    return x

_drawn_inputs = setup_inputs


def setup_inputs(seed=0):
    import zlib

    import numpy as np

    out = dict(_drawn_inputs(seed))
    spreads = {'L1_gnn_b_msg': (0.0, 0.1), 'L1_gnn_b_upd': (0.0, 0.382)}
    factors = {'edge_weight': 3.58, 'L0_gnn_b': 8.0}
    for name, (base, spread) in spreads.items():
        noise = np.random.default_rng([zlib.crc32(name.encode()), seed]).standard_normal(out[name].shape)
        drawn = base * np.exp(spread * noise) if base else spread * noise
        out[name] = jnp.asarray(drawn.astype(out[name].dtype))
    for name, factor in factors.items():
        out[name] = (out[name] * factor).astype(out[name].dtype)
    return out
```

```python
import concourse.bass as bass
from concourse import mybir
from contextlib import ExitStack


def two_layer_gnn(
    nc: bass.Bass,
    x: bass.AP,
    src: bass.AP,
    dst: bass.AP,
    edge_attr: bass.AP,
    edge_weight: bass.AP,
    W0: bass.AP,
    b0: bass.AP,
    W_msg: bass.AP,
    b_msg: bass.AP,
    W_upd: bass.AP,
    b_upd: bass.AP,
    eps: bass.AP,
    out: bass.AP,
):
    fp32 = mybir.dt.float32
    i32 = mybir.dt.int32
    u32 = mybir.dt.uint32
    ALU = mybir.AluOpType
    ACT = mybir.ActivationFunctionType
    AX = mybir.AxisListType

    N, D = x.shape
    E = src.shape[0]
    P = 128

    PN = 125
    KN = 5
    CHUNK = PN * KN
    NC = N // CHUNK
    assert NC * CHUNK == N

    J = 8
    G = P * J
    SLOTS = 4
    NG = -(-E // G)
    NG = -(-NG // SLOTS) * SLOTS
    BODIES = NG // SLOTS
    LAST = NG - 1
    assert (NG - 1) * G < E <= NG * G
    TWICE = NG * G - E
    assert TWICE % J == 0
    WIN = 128
    MAXW = -(-N // WIN)
    DA = D + 1
    HALF = (P, NG - P)
    LN_EPS = 1e-5
    DEG_EPS = 1e-6

    NK = NC * KN

    h0_table = nc.dram_tensor("h0_table", (N, D), fp32, kind="Internal").ap()
    p1_table = nc.dram_tensor("p1_table", (N, D), fp32, kind="Internal").ap()

    x_view = x.rearrange("(c p k) d -> p c (k d)", p=PN, k=KN)
    out_view = out.rearrange("(c p k) d -> p c (k d)", p=PN, k=KN)
    h0_view = h0_table.rearrange("(c p k) d -> p c (k d)", p=PN, k=KN)
    p1_view = p1_table.rearrange("(c p k) d -> p c (k d)", p=PN, k=KN)

    PARTS = 2
    PC = NC // PARTS

    ctx = ExitStack()
    with ctx:
        def sb(name, shape, dt=fp32):
            return ctx.enter_context(nc.sbuf_tensor(name, shape, dt))

        def sem(name):
            return ctx.enter_context(nc.semaphore(name))

        ident = sb("ident", [P, P])
        iota_i = sb("iota_i", [P, WIN], i32)
        iota = sb("iota", [P, WIN])
        ones_row = sb("ones_row", [1, P])
        W0_sb = sb("W0_sb", [DA, DA])
        W1a_sb = sb("W1a_sb", [DA, D])
        W1b_sb = sb("W1b_sb", [P, P])
        Wu_sb = sb("Wu_sb", [DA, D])
        eps_sb = sb("eps_sb", [D, 1])
        scale1 = sb("scale1", [D, 1])

        src_raw = sb("src_raw", [P, 2, G], i32)
        src_f = sb("src_f", [P, 2, G])
        dst_raw = sb("dst_raw", [P, 2, G], i32)
        dst_f = sb("dst_f", [P, 2, G])
        w_raw = sb("w_raw", [P, 2, G])
        src_tab = sb("src_tab", [P, NG * J], i32)
        dw_tab = sb("dw_tab", [P, NG, 2, J])
        stat = sb("stat", [P, 2, 4])
        stat_i = sb("stat_i", [P, 2, 1], i32)
        row_f = sb("row_f", [1, 3, NG])
        minus_row = sb("minus_row", [1, NG])
        row_i = sb("row_i", [1, NG, 4], i32)
        base_bc = sb("base_bc", [P, NG])

        x_sb = sb("x_sb", [PN, NC, KN * D])
        h_sb = sb("h_sb", [PN, NC, KN * D])
        sq = sb("sq", [PN, PC, KN * D])
        ln_m = sb("ln_m", [PN, 6, NK])
        deg = sb("deg", [PN, 2, KN])
        sums0 = sb("sums0", [DA, N + WIN])
        sums1 = sb("sums1", [DA, N + WIN])
        hT = sb("hT", [DA, 2, KN * PN])

        idx = sb("idx", [P, SLOTS, J], i32)
        rows = sb("rows", [P, SLOTS, J, DA])
        ea = sb("ea", [P, SLOTS, J * D])
        eT = sb("eT", [P, J // 2 * P])
        pre = sb("pre", [P, 2, J * D])
        msg = sb("msg", [P, 2, J * D])
        dw = sb("dw", [P, 2, 2, J])
        onehot = sb("onehot", [P, 2, J, WIN])
        tick = sb("tick", [1, SLOTS])

        ps = ctx.enter_context(nc.psum_tensor("ps", [P, 8, 512], fp32))
        psW = [ps[:, 0, 0:WIN], ps[:, 7, 0:WIN]]
        psT = ps[:, 1, :]
        psM = ps[:, 2, :]
        psR = [ps[:, 3:5, :], ps[:, 5:7, :]]
        psN = [ps[:, 1 + i, :] for i in range(2)]
        psS = ps[:, 7, :]

        s_w = sem("weights_loaded")
        s_x = sem("x_loaded")
        s_src = sem("src_loaded")
        s_dst = sem("dst_loaded")
        s_wt = sem("edge_weight_loaded")
        s_const = sem("constants_ready")
        s_zero = sem("buffers_set")
        s_identf = sem("identity_step")
        s_dvm = sem("edge_table_step")
        s_srcf = sem("src_is_float")
        s_dstf = sem("dst_is_float")
        s_tr = sem("edge_array_transposed")
        s_srct = sem("src_table_part")
        s_dwt = sem("target_weight_table_part")
        s_stats = sem("group_stats_ready")
        s_stat_t = sem("group_stats_transposed")
        s_rowf = sem("base_row_ready")
        s_base_ps = sem("base_broadcast")
        s_tables = sem("edge_tables_ready")
        s_ln = sem("layer_norm_step")
        s_sub = [sem("centred0"), sem("centred1")]
        s_sq = [sem("squared0"), sem("squared1")]
        s_var = [sem("variance0_ready"), sem("variance1_ready")]
        s_std = [sem("std0_ready"), sem("std1_ready")]
        s_h = [sem("h0_ready"), sem("h1_ready")]
        s_tabw = [[sem(f"table{n}_written{i}") for i in range(PARTS)] for n in range(2)]
        s_agg = sem("sums0_multiplied")
        s_x1 = sem("x1_ready")
        s_ht = sem("h1_transposed")
        s_htc = sem("h1_T_copied")
        s_seed = sem("sums1_seeded")
        s_tab = sem("table1_multiplied")
        s_tabc = sem("table1_copied")
        s_idx = [sem(f"idx_ready{s}") for s in range(SLOTS)]
        s_gat = [sem(f"gathered{s}") for s in range(SLOTS)]
        s_ea = [sem(f"edge_attr_loaded{s}") for s in range(SLOTS)]
        s_dw = [sem("dw0_ready"), sem("dw1_ready")]
        s_oh = [sem("onehot0_ready"), sem("onehot1_ready")]
        s_win = [sem("window0_summed"), sem("window1_summed")]
        s_acc = [sem("window0_added"), sem("window1_added")]
        s_more_dw = [sem("more_dw0_ready"), sem("more_dw1_ready")]
        s_more_oh = [sem("more_onehot0_ready"), sem("more_onehot1_ready")]
        s_more_win = [sem("more_window0_summed"), sem("more_window1_summed")]
        s_more_acc = [sem("more_window0_added"), sem("more_window1_added")]
        s_done = sem("group1_summed")
        s_passed = sem("waits_passed")
        s_et = sem("edge_attr_transposed")
        s_etc = sem("edge_attr_T_copied")
        s_em = sem("edge_attr_multiplied")
        s_used = [sem(f"rows_used{s}") for s in range(SLOTS)]
        s_msg = sem("message_ready")
        s_fin_mm = sem("update_multiplied")
        s_fin_g = sem("update_gelu")
        s_fin = sem("update_added")
        s_out = sem("out_written")

        block = ctx.enter_context(nc.Block())

        def part(t, n):
            return t[:, n * PC:(n + 1) * PC, :]

        @block.sync
        def _(sp):
            for one in s_used:
                sp.sem_inc(one, 1)
            for one in (s_msg, s_done, *s_acc):
                sp.sem_inc(one, 2)
            sp.dma_start(x_sb[:, :, :], x_view).then_inc(s_x, 16)

            def load_edges(to, a, loaded):
                sp.dma_start(to[:, 0, :], a[0:P * G].rearrange("(r e) -> r e", e=G)).then_inc(loaded, 16)
                sp.dma_start(to[0:HALF[1] - 1, 1, :],
                             a[P * G:LAST * G].rearrange("(r e) -> r e", e=G)).then_inc(loaded, 16)
                sp.dma_start(to[HALF[1] - 1:HALF[1], 1, :],
                             a[E - G:E].rearrange("(r e) -> r e", e=G)).then_inc(loaded, 16)

            load_edges(src_raw, src, s_src)
            load_edges(dst_raw, dst, s_dst)
            load_edges(w_raw, edge_weight, s_wt)
            for n in range(PARTS):
                sp.wait_ge(s_h[0], n + 1)
                sp.dma_start(part(h0_view, n), part(h_sb, n)).then_inc(s_tabw[0][n], 16)
            sp.wait_ge(s_const, 5)
            sp.dma_start(W0_sb[0:D, 0:D], W0).then_inc(s_w, 16)
            sp.dma_start(W0_sb[D:DA, 0:D], b0.rearrange("(a n) -> a n", a=1)).then_inc(s_w, 16)
            sp.dma_start(W1a_sb[0:D, :], W_msg[0:D, :]).then_inc(s_w, 16)
            sp.dma_start(W1a_sb[D:DA, :], b_msg.rearrange("(a n) -> a n", a=1)).then_inc(s_w, 16)
            for h in range(2):
                sp.dma_start(W1b_sb[h * D:(h + 1) * D, h * D:(h + 1) * D], W_msg[D:2 * D, :]).then_inc(s_w, 16)
            sp.dma_start(Wu_sb[0:D, :], W_upd).then_inc(s_w, 16)
            sp.dma_start(Wu_sb[D:DA, :], b_upd.rearrange("(a n) -> a n", a=1)).then_inc(s_w, 16)
            sp.dma_start(eps_sb[:, :], eps.rearrange("(a n) -> a n", a=1).to_broadcast([D, 1])).then_inc(s_w, 16)

            def load_ea(g, s):
                at = E - G if isinstance(g, int) and g == LAST else g * G
                v = edge_attr[bass.ds(at, G), :].rearrange("(p j) d -> p (j d)", j=J)
                sp.dma_start(ea[:, s, :], v).then_inc(s_ea[s], 16)

            for s in range(SLOTS):
                load_ea(s, s)
            for n in range(PARTS):
                sp.wait_ge(s_tabc, PC * (n + 1))
                sp.dma_start(part(p1_view, n), part(h_sb, n)).then_inc(s_tabw[1][n], 16)
            with sp.Fori(0, BODIES - 2) as b:
                for s in range(SLOTS):
                    sp.wait_ge(s_et, b * SLOTS + (s + 1))
                    load_ea((b + 1) * SLOTS + s, s)
            for s in range(SLOTS):
                sp.wait_ge(s_et, (BODIES - 2) * SLOTS + s + 1)
                load_ea((BODIES - 1) * SLOTS + s, s)
            for c in range(0, NC, 2):
                sp.wait_ge(s_fin, c + 2)
                sp.dma_start(out_view[:, c:c + 2, :], h_sb[:, c:c + 2, :]).then_inc(s_out, 16)
            sp.wait_ge(s_out, NC // 2 * 16)

        @block.gpsimd
        def _(pool):
            nc.gpsimd.memset(ident[:, :], 0.0).then_inc(s_identf, 1)
            pool.wait_ge(s_identf, 1)
            nc.gpsimd.affine_select(out=ident[:, :], in_=ident[:, :], compare_op=ALU.not_equal, fill=1.0,
                                    base=0, pattern=[[-1, P]], channel_multiplier=1).then_inc(s_const, 1)
            nc.gpsimd.iota(iota_i[:, :], pattern=[[1, WIN]], base=0, channel_multiplier=0).then_inc(s_const, 1)
            nc.gpsimd.memset(rows[:, :, :, D:DA], 1.0).then_inc(s_const, 1)
            for layer, table in ((0, h0_table), (1, p1_table)):
                for n in range(PARTS):
                    pool.wait_ge(s_tabw[layer][n], 16)
                with pool.Fori(layer * BODIES + 1, (layer + 1) * BODIES + 1) as turn:
                    for s in range(SLOTS):
                        pool.wait_ge(s_const, 5)
                        pool.wait_ge(s_idx[s], turn)
                        pool.wait_ge(s_used[s], turn)
                        for j in range(J):
                            nc.gpsimd.indirect_dma_start(
                                out=rows[:, s, j, 0:D], out_offset=None, in_=table[:, :],
                                in_offset=bass.IndirectOffsetOnAxis(ap=idx[:, s, j:j + 1].bitcast(u32), axis=0),
                            ).then_inc(s_gat[s], 16)

        @block.scalar
        def _(act):
            def copy_idx(g, s):
                nc.scalar.copy(idx[:, s, :], src_tab[:, bass.ds(g * J, J)]).then_inc(s_idx[s], 1)

            def norm(layer):
                for n in range(PARTS):
                    act.wait_ge(s_sub[layer], n + 1)
                    if n:
                        act.wait_ge(s_var[layer], n)
                    nc.scalar.activation(sq[:, :, :], part(h_sb, n), ACT.Square).then_inc(s_sq[layer], 1)
                for n in range(PARTS):
                    at = slice(n * PC * KN, (n + 1) * PC * KN)
                    act.wait_ge(s_var[layer], n + 1)
                    nc.scalar.activation(ln_m[:, 3, at], ln_m[:, 2, at], ACT.Sqrt).then_inc(s_std[layer], 1)

            norm(0)
            act.wait_ge(s_src, 48)
            nc.scalar.copy(src_f[:, 0, :], src_raw[:, 0, :])
            nc.scalar.copy(src_f[0:HALF[1], 1, :], src_raw[0:HALF[1], 1, :]).then_inc(s_srcf, 1)
            for half in range(2):
                r = HALF[half]
                act.wait_ge(s_tr, half + 1)
                for m in range(2):
                    last = nc.scalar.copy(
                        src_tab[:, :].rearrange("p (g j) -> p j g", j=J)[:, 4 * m:4 * m + 4, half * P:half * P + r],
                        psR[half % 2][:, m, :].rearrange("p (j g) -> p j g", g=P)[:, :, 0:r])
                last.then_inc(s_srct, 1)
            act.wait_ge(s_srct, 2)
            for s in range(SLOTS):
                copy_idx(s, s)
            with act.Fori(0, BODIES - 1) as b:
                for s in range(SLOTS):
                    act.wait_ge(s_gat[s], (b + 1) * (16 * J))
                    copy_idx((b + 1) * SLOTS + s, s)
            for s in range(SLOTS):
                act.wait_ge(s_gat[s], BODIES * 16 * J)
                copy_idx(s, s)
            norm(1)
            for c in range(NC):
                act.wait_ge(s_ht, c + 1)
                if c >= 2:
                    act.wait_ge(s_tab, c - 1)
                    act.wait_ge(s_seed, c - 1)
                nc.scalar.copy(hT[0:D, c % 2, 0:4 * PN], psR[c % 2][0:D, 0, 0:4 * PN])
                nc.scalar.copy(hT[0:D, c % 2, 4 * PN:5 * PN], psR[c % 2][0:D, 1, 0:PN]).then_inc(s_htc, 1)
                act.wait_ge(s_tab, c + 1)
                nc.scalar.copy(h_sb[:, c, :], psN[c % 2][0:PN, 0:KN * D]).then_inc(s_tabc, 1)

            def message(b, s):
                act.wait_ge(s_et, b * SLOTS + (s + 1))
                nc.scalar.copy(eT[:, :], psT[:, :]).then_inc(s_etc, 1)
                act.wait_ge(s_used[s], b + (1 + BODIES + 1))
                act.wait_ge(s_done, b * SLOTS + (s + 1))
                nc.scalar.activation(msg[:, s % 2, :], pre[:, s % 2, :], ACT.Gelu_apprx_tanh).then_inc(s_msg, 1)

            with act.Fori(0, BODIES - 1) as b:
                for s in range(SLOTS):
                    message(b, s)
                    copy_idx((b + 1) * SLOTS + s, s)
            for s in range(SLOTS):
                message(BODIES - 1, s)
            for c in range(NC):
                act.wait_ge(s_fin_mm, c + 1)
                nc.scalar.activation(h_sb[:, c, :], psN[c % 2][0:PN, 0:KN * D], ACT.Gelu_apprx_tanh).then_inc(s_fin_g, 1)

        @block.tensor
        def _(pe):
            pe.wait_ge(s_const, 5)

            def turn(a, half, to):
                r = HALF[half]
                v = a[0:r, half, :].rearrange("r (p j) -> r j p", j=J)
                for j in range(J):
                    last = nc.tensor.transpose(to[:, j // 4, (j % 4) * P:(j % 4) * P + r],
                                               v[:, j, :], ident[0:r, 0:r])
                last.then_inc(s_tr, 1)

            pe.wait_ge(s_srcf, 1)
            turn(src_f, 0, psR[0])
            turn(src_f, 1, psR[1])
            pe.wait_ge(s_stats, 1)
            for half in range(2):
                r = HALF[half]
                for q in range(2):
                    last = nc.tensor.transpose(psS[0:1, q * 256 + half * P:q * 256 + half * P + r],
                                               stat[0:r, half, q * 3:q * 3 + 1], ident[0:r, 0:r])
            last.then_inc(s_stat_t, 1)
            pe.wait_ge(s_srct, 1)
            turn(dst_f, 0, psR[0])
            pe.wait_ge(s_srct, 2)
            turn(dst_f, 1, psR[1])
            pe.wait_ge(s_rowf, 1)
            nc.tensor.matmul(psS[:, 0:NG], ones_row[:, :], row_f[:, 0, :],
                             start=True, stop=True).then_inc(s_base_ps, 1)
            pe.wait_ge(s_wt, 48)
            for half in range(2):
                pe.wait_ge(s_dwt, half + 1)
                turn(w_raw, half, psR[half])

            def windows(layer, b, s, lhs, width):
                g = b * SLOTS + s
                pe.wait_ge(s_oh[layer], b * SLOTS + (s + 1))
                pe.wait_ge(s_acc[layer], b * SLOTS + (s + 1))

                def product(done):
                    for j in range(J):
                        last = nc.tensor.matmul(psW[s % 2][0:width, :], lhs(j), onehot[:, s % 2, j, :],
                                                start=(j == 0), stop=(j == J - 1))
                    last.then_inc(done[layer], 1)

                product(s_win)
                count = pe.value_load(row_i[0:1, bass.ds(g, 1), 1], min_val=1, max_val=MAXW)
                with pe.If(count > 1):
                    before = pe.value_load(row_i[0:1, bass.ds(g, 1), 2], min_val=0, max_val=MAXW * NG)
                    with pe.Fori(0, count - 1) as i:
                        pe.wait_ge(s_more_oh[layer], before + i + 1)
                        product(s_more_win)

            pe.wait_ge(s_tables, 1)
            with pe.Fori(0, BODIES) as b:
                for s in range(SLOTS):
                    pe.wait_ge(s_gat[s], (b + 1) * (16 * J))
                    windows(0, b, s, lambda j, s=s: rows[:, s, j, :], DA)

            for s in range(SLOTS):
                pe.wait_ge(s_used[s], BODIES + 1)
            pe.wait_ge(s_acc[0], NG + 2)
            pe.wait_ge(s_w, 16 * 9)

            def sums_product(sums, c, W, width, done):
                v = sums[:, c * CHUNK:(c + 1) * CHUNK].rearrange("f (p k) -> f k p", k=KN)
                for k in range(KN):
                    last = nc.tensor.matmul(psN[c % 2][0:PN, k * width:(k + 1) * width], v[:, k, :], W,
                                            start=True, stop=True)
                last.then_inc(done, 1)

            for c in range(NC):
                if c >= 2:
                    pe.wait_ge(s_x1, c - 1)
                sums_product(sums0, c, W0_sb[:, :], DA, s_agg)
            for c in range(NC + 1):
                if c < NC:
                    pe.wait_ge(s_h[1], c // PC + 1)
                    if c >= 2:
                        pe.wait_ge(s_htc, c - 1)
                    for k in range(KN):
                        last = nc.tensor.transpose(psR[c % 2][0:D, k // 4, k % 4 * PN:(k % 4 + 1) * PN],
                                                   h_sb[:, c, k * D:(k + 1) * D], ident[0:PN, 0:PN])
                    last.then_inc(s_ht, 1)
                if c:
                    n = c - 1
                    pe.wait_ge(s_htc, n + 1)
                    if n >= 2:
                        pe.wait_ge(s_tabc, n - 1)
                    for k in range(KN):
                        last = nc.tensor.matmul(psN[n % 2][0:PN, k * D:(k + 1) * D],
                                                hT[:, n % 2, k * PN:(k + 1) * PN], W1a_sb[:, :],
                                                start=True, stop=True)
                    last.then_inc(s_tab, 1)

            def edge_product(b, s, shift):
                slot = (s + shift) % SLOTS
                g = b * SLOTS + (s + shift)
                pe.wait_ge(s_ea[slot], (b + (s + shift) // SLOTS + 1) * 16)
                if shift:
                    pe.wait_ge(s_etc, g)
                for q in range(J // 2):
                    last = nc.tensor.transpose(psT[:, q * P:(q + 1) * P], ea[:, slot, q * P:(q + 1) * P],
                                               ident[:, :])
                last.then_inc(s_et, 1)
                pe.wait_ge(s_etc, g + 1)
                if shift:
                    pe.wait_ge(s_used[s], b + (1 + BODIES + 1))
                for q in range(J // 2):
                    last = nc.tensor.matmul(psM[:, q * P:(q + 1) * P], eT[:, q * P:(q + 1) * P],
                                            W1b_sb[:, :], start=True, stop=True)
                last.then_inc(s_em, 1)

            pe.wait_ge(s_tabc, NC)
            edge_product(0, 0, 0)

            def second(b, last_body):
                for s in range(SLOTS):
                    if not (last_body and s == SLOTS - 1):
                        edge_product(b, s, 1)
                    pe.wait_ge(s_msg, b * SLOTS + (s + 1 + 2))
                    windows(1, b, s, lambda j, s=s: msg[:, s % 2, j * D:(j + 1) * D], D)

            with pe.Fori(0, BODIES - 1) as b:
                second(b, False)
            second(BODIES - 1, True)

            pe.wait_ge(s_done, NG + 2)
            pe.wait_ge(s_acc[1], NG + 2)
            for c in range(NC):
                if c >= 2:
                    pe.wait_ge(s_fin_g, c - 1)
                sums_product(sums1, c, Wu_sb[:, :], D, s_fin_mm)

        @block.vector
        def _(dve):
            at = [0, 0]

            def meta(ins):
                at[0] += 1
                ins.then_inc(s_dvm, 1)
                dve.wait_ge(s_dvm, at[0])

            def step(ins):
                at[1] += 1
                ins.then_inc(s_ln, 1)
                dve.wait_ge(s_ln, at[1])

            nc.vector.memset(W1b_sb[:, :], 0.0).then_inc(s_const, 1)
            step(nc.vector.memset(W0_sb[:, :], 0.0))
            nc.vector.memset(W0_sb[D:DA, D:DA], 1.0)
            nc.vector.memset(ones_row[:, :], 1.0).then_inc(s_const, 1)

            def k3(t):
                return t.rearrange("p c (k d) -> p (c k) d", d=D)

            def layer_norm(layer):
                def m(q, n):
                    return ln_m[:, q, n * PC * KN:(n + 1) * PC * KN]

                def mb(q, n):
                    return m(q, n).unsqueeze(2).to_broadcast([PN, PC * KN, D])

                for n in range(PARTS):
                    step(nc.vector.tensor_reduce(m(0, n), k3(part(x_sb, n)), AX.X, ALU.add))
                    step(nc.vector.tensor_scalar(m(1, n), m(0, n), 1.0 / D, None, ALU.mult))
                    nc.vector.tensor_tensor(k3(part(h_sb, n)), k3(part(x_sb, n)), mb(1, n),
                                            ALU.subtract).then_inc(s_sub[layer], 1)
                for n in range(PARTS):
                    dve.wait_ge(s_sq[layer], n + 1)
                    step(nc.vector.tensor_reduce(m(4, n), k3(sq[:, :, :]), AX.X, ALU.add))
                    nc.vector.tensor_scalar(m(2, n), m(4, n), 1.0 / D, LN_EPS,
                                            ALU.mult, ALU.add).then_inc(s_var[layer], 1)
                for n in range(PARTS):
                    dve.wait_ge(s_std[layer], n + 1)
                    step(nc.vector.reciprocal(m(5, n), m(3, n)))
                    nc.vector.scalar_tensor_tensor(out=k3(part(h_sb, n)), in0=k3(part(h_sb, n)), scalar=0.0,
                                                   in1=mb(5, n), op0=ALU.max, op1=ALU.mult).then_inc(s_h[layer], 1)

            dve.wait_ge(s_x, 16)
            layer_norm(0)

            dve.wait_ge(s_const, 5)
            meta(nc.vector.tensor_copy(iota[:, :], iota_i[:, :]))
            nc.vector.memset(sums0[:, :], 0.0).then_inc(s_zero, 1)
            nc.vector.memset(sums1[D:DA, :], 1.0)
            nc.vector.memset(sums1[0:D, N:N + WIN], 0.0)
            nc.vector.memset(hT[D:DA, :, :], 1.0)
            meta(nc.vector.memset(minus_row[:, :], -1.0))

            dve.wait_ge(s_dst, 48)
            nc.vector.tensor_copy(dst_f[:, 0, :], dst_raw[:, 0, :])
            meta(nc.vector.tensor_copy(dst_f[0:HALF[1], 1, :], dst_raw[0:HALF[1], 1, :]))
            for half in range(2):
                r = HALF[half]
                nc.vector.tensor_reduce(stat[0:r, half, 0:1], dst_f[0:r, half, :], AX.X, ALU.min)
                meta(nc.vector.tensor_reduce(stat[0:r, half, 1:2], dst_f[0:r, half, :], AX.X, ALU.max))
                meta(nc.vector.tensor_tensor(stat[0:r, half, 2:3], stat[0:r, half, 1:2], stat[0:r, half, 0:1],
                                             ALU.subtract))
                meta(nc.vector.tensor_copy(stat_i[0:r, half, :], stat[0:r, half, 2:3]))
                meta(nc.vector.tensor_scalar(stat_i[0:r, half, :], stat_i[0:r, half, :], 7, None,
                                             ALU.logical_shift_right))
                last = nc.vector.tensor_scalar_add(stat[0:r, half, 3:4], stat_i[0:r, half, :], 1.0)
            last.then_inc(s_stats, 1)

            def take(first, to):
                for half in range(2):
                    r = HALF[half]
                    dve.wait_ge(s_tr, first + half + 1)
                    for m in range(2):
                        last = nc.vector.tensor_copy(
                            to[:, half * P:half * P + r, 4 * m:4 * m + 4].rearrange("p g j -> p j g"),
                            psR[half][:, m, :].rearrange("p (j g) -> p j g", g=P)[:, :, 0:r])
                    last.then_inc(s_dwt, 1)

            dve.wait_ge(s_stat_t, 1)
            meta(nc.vector.tensor_copy(row_f[:, 0:2, :],
                                       psS[0:1, :].rearrange("a (q g) -> a q g", q=2)[:, :, 0:NG]))
            nc.vector.tensor_tensor_scan(row_f[:, 2, :], row_f[:, 1, :], minus_row[:, :], 0.0,
                                         ALU.add, ALU.add).then_inc(s_rowf, 1)
            dve.wait_ge(s_rowf, 1)
            meta(nc.vector.scalar_tensor_tensor(out=row_f[:, 2, :], in0=row_f[:, 2, :], scalar=1.0,
                                                in1=row_f[:, 1, :], op0=ALU.add, op1=ALU.subtract))
            meta(nc.vector.tensor_copy(row_i[:, :, 0:3].rearrange("a g q -> a q g"), row_f[:, :, :]))
            take(2, dw_tab[:, :, 0, :])
            dve.wait_ge(s_base_ps, 1)
            meta(nc.vector.tensor_copy(base_bc[:, :], psS[:, 0:NG]))
            dve.wait_ge(s_dwt, 2)
            meta(nc.vector.tensor_tensor(dw_tab[:, :, 0, :], dw_tab[:, :, 0, :],
                                         base_bc[:, :].unsqueeze(2).to_broadcast([P, NG, J]), ALU.subtract))
            meta(nc.vector.memset(dw_tab[0:TWICE // J, LAST, 0, :], -1e6))
            take(4, dw_tab[:, :, 1, :])
            dve.wait_ge(s_dwt, 4)
            nc.vector.memset(tick[:, :], 0.0).then_inc(s_tables, 1)

            def onehots(layer, par, done):
                for j in range(J):
                    if layer == 0:
                        last = nc.vector.tensor_scalar(onehot[:, par, j, :], iota[:, :], dw[:, par, 0, j:j + 1],
                                                       dw[:, par, 1, j:j + 1], ALU.is_equal, ALU.mult)
                    else:
                        last = nc.vector.tensor_scalar(onehot[:, par, j, :], iota[:, :], dw[:, par, 0, j:j + 1],
                                                       None, ALU.is_equal)
                last.then_inc(done, 1)

            def first_onehots(layer, b, s, shift):
                g = b * SLOTS + (s + shift)
                par = (s + shift) % 2
                nc.vector.tensor_copy(dw[:, par, :, :], dw_tab[:, bass.ds(g, 1), :, :].rearrange(
                    "p a q j -> p (a q) j")).then_inc(s_dw[layer], 1)
                dve.wait_ge(s_dw[layer], b * SLOTS + (s + shift + 1))
                onehots(layer, par, s_oh[layer])

            def sums(layer, b, s, width):
                g = b * SLOTS + s
                par = s % 2
                base = dve.value_load(row_i[0:1, bass.ds(g, 1), 0], min_val=0, max_val=N - 1)
                count = dve.value_load(row_i[0:1, bass.ds(g, 1), 1], min_val=1, max_val=MAXW)
                dve.wait_ge(s_win[layer], b * SLOTS + (s + 1))
                dve.wait_ge(s_acc[layer], b * SLOTS + (s + 2))
                to = (sums0, sums1)[layer][0:width, bass.ds(base, WIN)]
                nc.vector.tensor_tensor(to, to, psW[par][0:width, :], ALU.add).then_inc(s_acc[layer], 1)
                with dve.If(count > 1):
                    before = dve.value_load(row_i[0:1, bass.ds(g, 1), 2], min_val=0, max_val=MAXW * NG)
                    dve.wait_ge(s_acc[layer], b * SLOTS + (s + 3))
                    dve.sem_inc(s_passed, 1)
                    with dve.Fori(0, count - 1) as i:
                        k = before + i + 1
                        nc.vector.tensor_scalar_add(dw[:, par, 0, :], dw[:, par, 0, :],
                                                    -float(WIN)).then_inc(s_more_dw[layer], 1)
                        dve.wait_ge(s_more_dw[layer], k)
                        onehots(layer, par, s_more_oh[layer])
                        dve.wait_ge(s_more_win[layer], k)
                        at_node = nc.s_assert_within(base + i * WIN + WIN, 0, N - 1, skip_runtime_bounds_check_because=(
                            "a group has just enough windows to reach its greatest target, which is below N"))
                        to = (sums0, sums1)[layer][0:width, bass.ds(at_node, WIN)]
                        nc.vector.tensor_tensor(to, to, psW[par][0:width, :], ALU.add).then_inc(s_more_acc[layer], 1)
                        dve.wait_ge(s_more_acc[layer], k)
                nc.vector.memset(tick[:, s:s + 1], 0.0).then_inc(s_used[s] if layer == 0 else s_done, 1)

            dve.wait_ge(s_zero, 1)
            first_onehots(0, 0, 0, 0)

            def first(b, last_body):
                for s in range(SLOTS):
                    if not (last_body and s == SLOTS - 1):
                        first_onehots(0, b, s, 1)
                    sums(0, b, s, DA)

            with dve.Fori(0, BODIES - 1) as b:
                first(b, False)
            first(BODIES - 1, True)

            for c in range(NC):
                dve.wait_ge(s_agg, c + 1)
                agg = psN[c % 2][0:PN, 0:KN * DA].rearrange("p (k f) -> p k f", f=DA)
                xc = x_sb[:, c, :].rearrange("p (k d) -> p k d", d=D)
                hc = h_sb[:, c, :].rearrange("p (k d) -> p k d", d=D)
                step(nc.vector.tensor_scalar_add(deg[:, 0, :], agg[:, :, D], DEG_EPS))
                step(nc.vector.reciprocal(deg[:, 1, :], deg[:, 0, :]))
                step(nc.vector.tensor_tensor(hc, agg[:, :, 0:D],
                                             deg[:, 1, :].unsqueeze(2).to_broadcast([PN, KN, D]), ALU.mult))
                nc.vector.scalar_tensor_tensor(out=xc, in0=hc, scalar=0.0, in1=xc,
                                               op0=ALU.max, op1=ALU.add).then_inc(s_x1, 1)
            dve.wait_ge(s_x1, NC)
            layer_norm(1)
            step(nc.vector.tensor_scalar_add(scale1[:, :], eps_sb[:, :], 1.0))
            for c in range(NC):
                dve.wait_ge(s_htc, c + 1)
                v = sums1[0:D, c * CHUNK:(c + 1) * CHUNK].rearrange("f (p k) -> f k p", k=KN)
                nc.vector.tensor_scalar(v, hT[0:D, c % 2, :].rearrange("f (k p) -> f k p", k=KN),
                                        scale1[:, 0:1], None, ALU.mult).then_inc(s_seed, 1)
            dve.wait_ge(s_seed, NC)

            def message_sum(b, s, shift):
                slot = (s + shift) % SLOTS
                g = b * SLOTS + (s + shift)
                dve.wait_ge(s_em, g + 1)
                dve.wait_ge(s_gat[slot], BODIES * 16 * J + (b + (s + shift) // SLOTS + 1) * (16 * J))
                dve.wait_ge(s_msg, g + 1)
                nc.vector.tensor_tensor(pre[:, slot % 2, :].rearrange("p (j d) -> p j d", d=D),
                                        psM.rearrange("p (j d) -> p j d", d=D), rows[:, slot, :, 0:D],
                                        ALU.add).then_inc(s_used[slot], 1)

            first_onehots(1, 0, 0, 0)
            message_sum(0, 0, 0)

            def second(b, last_body):
                for s in range(SLOTS):
                    if not (last_body and s == SLOTS - 1):
                        first_onehots(1, b, s, 1)
                        message_sum(b, s, 1)
                    sums(1, b, s, D)

            with dve.Fori(0, BODIES - 1) as b:
                second(b, False)
            second(BODIES - 1, True)

            for c in range(NC):
                dve.wait_ge(s_fin_g, c + 1)
                nc.vector.tensor_tensor(h_sb[:, c, :], h_sb[:, c, :], x_sb[:, c, :], ALU.add).then_inc(s_fin, 1)


_INS = ["x", "src", "dst", "edge_attr_64", "edge_weight", "L0_gnn_W", "L0_gnn_b", "L1_gnn_W_msg",
        "L1_gnn_b_msg", "L1_gnn_W_upd", "L1_gnn_b_upd", "L1_gnn_eps"]
_OUTS = [((6250, 64), "float32")]


def kernel(**inputs):
    import numpy as _np
    import concourse.bacc as _bacc
    from concourse import mybir as _mybir
    from concourse.bass_utils import run_bass_kernel_spmd as _run

    nc = _bacc.Bacc("TRN2", target_bir_lowering=False, num_devices=1)
    arrays, args = {}, []
    for name in _INS:
        a = _np.ascontiguousarray(inputs[name])
        arrays[f"in_{name}_dram"] = a
        args.append(nc.dram_tensor(f"in_{name}_dram", a.shape, _mybir.dt.from_np(a.dtype), kind="ExternalInput").ap())
    for i, (shape, dtype) in enumerate(_OUTS):
        dt = _mybir.dt.from_np(_np.dtype(dtype))
        args.append(nc.dram_tensor(f"out_{i}_dram", shape, dt, kind="ExternalOutput").ap())
    two_layer_gnn(nc, *args)
    r = _run(nc, [arrays], core_ids=[0])
    got = tuple(r.results[0][f"out_{i}_dram"] for i in range(len(_OUTS)))
    return got[0]
```

```python
import concourse.bass as bass
from concourse import mybir
from contextlib import ExitStack


def two_layer_gnn(
    nc: bass.Bass,
    x: bass.AP,
    src: bass.AP,
    dst: bass.AP,
    edge_attr: bass.AP,
    edge_weight: bass.AP,
    W0: bass.AP,
    b0: bass.AP,
    W_msg: bass.AP,
    b_msg: bass.AP,
    W_upd: bass.AP,
    b_upd: bass.AP,
    eps: bass.AP,
    out: bass.AP,
):
    fp32 = mybir.dt.float32
    i32 = mybir.dt.int32
    u16 = mybir.dt.uint16
    i16 = mybir.dt.int16
    bf16 = mybir.dt.bfloat16
    u32 = mybir.dt.uint32
    ALU = mybir.AluOpType
    ACT = mybir.ActivationFunctionType
    AX = mybir.AxisListType

    N, D = x.shape
    E = src.shape[0]
    P = 128

    PN = 125
    KN = 5
    CHUNK = PN * KN
    NC = N // CHUNK
    assert NC * CHUNK == N

    J = 8
    G = P * J
    SLOTS = 4
    NG = -(-E // G)
    NG = -(-NG // SLOTS) * SLOTS
    BODIES = NG // SLOTS
    LAST = NG - 1
    assert (NG - 1) * G < E <= NG * G
    TWICE = NG * G - E
    assert TWICE % J == 0
    WIN = 128
    MAXW = -(-N // WIN)
    DA = D + 1
    HALF = (P, NG - P)
    LN_EPS = 1e-5
    DEG_EPS = 1e-6

    NK = NC * KN

    JG = J - 1
    SPLIT = 3
    PAIRS = NG // 2
    PE2 = 2 * P

    h0_table = nc.dram_tensor("h0_table", (N, D), fp32, kind="Internal").ap()
    p1_table = nc.dram_tensor("p1_table", (N, D), fp32, kind="Internal").ap()
    last_src = nc.dram_tensor("last_src", (NG, P), u16, kind="Internal").ap()

    x_view = x.rearrange("(c p k) d -> p c (k d)", p=PN, k=KN)
    out_view = out.rearrange("(c p k) d -> p c (k d)", p=PN, k=KN)
    h0_view = h0_table.rearrange("(c p k) d -> p c (k d)", p=PN, k=KN)
    p1_view = p1_table.rearrange("(c p k) d -> p c (k d)", p=PN, k=KN)

    PARTS = 2
    PC = NC // PARTS

    ctx = ExitStack()
    with ctx:
        def sb(name, shape, dt=fp32):
            return ctx.enter_context(nc.sbuf_tensor(name, shape, dt))

        def sem(name):
            return ctx.enter_context(nc.semaphore(name))

        ident = sb("ident", [P, P])
        iota_i = sb("iota_i", [P, WIN], i32)
        iota = sb("iota", [P, WIN])
        ones_row = sb("ones_row", [1, P])
        W0_sb = sb("W0_sb", [DA, DA])
        W1a_sb = sb("W1a_sb", [DA, D])
        W1b_sb = sb("W1b_sb", [P, P])
        Wu_sb = sb("Wu_sb", [DA, D])
        eps_sb = sb("eps_sb", [D, 1])
        scale1 = sb("scale1", [D, 1])

        node_i = sb("node_i", [PN, 1], i32)
        node_f = sb("node_f", [PN, 1])
        parts = sb("parts", [PN, NK, SPLIT * D], bf16)
        src_bc = sb("src_bc", [PN, 2, PE2], u16)
        src_off = sb("src_off", [PN, PE2], i16)
        pick = sb("pick", [P, 2, NK, PE2], bf16)

        flat_f = pick[:, :, :, :].rearrange("p a b e -> p (a b e)").bitcast(fp32)
        flat_i = pick[:, :, :, :].rearrange("p a b e -> p (a b e)").bitcast(i32)

        def prep(flat, n):
            return flat[:, n * 2 * G:(n + 1) * 2 * G].rearrange("p (h e) -> p h e", h=2)

        src_raw, dst_raw = prep(flat_i, 0), prep(flat_i, 1)
        src_f, dst_f, w_raw = prep(flat_f, 2), prep(flat_f, 3), prep(flat_f, 4)
        src_last = sb("src_last", [P, 2, P], u16)
        src_tab = sb("src_tab", [P, NG * J], i32)
        dw_tab = sb("dw_tab", [P, NG, 2, J])
        stat = sb("stat", [P, 2, 4])
        stat_i = sb("stat_i", [P, 2, 1], i32)
        row_f = sb("row_f", [1, 3, NG])
        minus_row = sb("minus_row", [1, NG])
        row_i = sb("row_i", [1, NG, 4], i32)
        base_bc = sb("base_bc", [P, NG])

        x_sb = sb("x_sb", [PN, NC, KN * D])
        h_sb = sb("h_sb", [PN, NC, KN * D])
        sq = sb("sq", [PN, PC, KN * D])
        ln_m = sb("ln_m", [PN, 6, NK])
        deg = sb("deg", [PN, 2, KN])
        sums_sb = sb("sums_sb", [DA, N + WIN])
        hT = sb("hT", [DA, 2, KN * PN])

        idx = sb("idx", [P, SLOTS, J], i32)
        rows = sb("rows", [P, SLOTS, J, DA])
        ea = sb("ea", [P, SLOTS, J * D])
        eT = sb("eT", [P, J // 2 * P])
        pre = sb("pre", [P, 2, J * D])
        msg = sb("msg", [P, 2, J * D])
        dw = sb("dw", [P, 2, 2, J])
        onehot = sb("onehot", [P, 2, J, WIN])
        tick = sb("tick", [1, SLOTS])

        ps = ctx.enter_context(nc.psum_tensor("ps", [P, 8, 512], fp32))
        psW = [ps[:, 0, 0:WIN], ps[:, 7, 0:WIN]]
        psT = ps[:, 1, :]
        psM = ps[:, 2, :]
        psR = [ps[:, 3:5, :], ps[:, 5:7, :]]
        psN = [ps[:, 1 + i, :] for i in range(2)]
        psS = ps[:, 7, :]
        psG = [ps[:, 3 + i, 0:SPLIT * D] for i in range(2)]

        s_w = sem("weights_loaded")
        s_x = sem("x_loaded")
        s_src = sem("src_loaded")
        s_dst = sem("dst_loaded")
        s_wt = sem("edge_weight_loaded")
        s_const = sem("constants_ready")
        s_zero = sem("buffers_set")
        s_identf = sem("identity_step")
        s_dvm = sem("edge_table_step")
        s_srcf = sem("src_is_float")
        s_dstf = sem("dst_is_float")
        s_tr = sem("edge_array_transposed")
        s_srct = sem("src_table_part")
        s_dwt = sem("target_weight_table_part")
        s_stats = sem("group_stats_ready")
        s_stat_t = sem("group_stats_transposed")
        s_rowf = sem("base_row_ready")
        s_base_ps = sem("base_broadcast")
        s_tables = sem("edge_tables_ready")
        s_ln = sem("layer_norm_step")
        s_sub = [sem("centred0"), sem("centred1")]
        s_sq = [sem("squared0"), sem("squared1")]
        s_var = [sem("variance0_ready"), sem("variance1_ready")]
        s_std = [sem("std0_ready"), sem("std1_ready")]
        s_h = [sem("h0_ready"), sem("h1_ready")]
        s_tabw = [[sem(f"table{n}_written{i}") for i in range(PARTS)] for n in range(2)]
        s_agg = sem("sums0_multiplied")
        s_x1 = sem("x1_ready")
        s_ht = sem("h1_transposed")
        s_htc = sem("h1_T_copied")
        s_seed = sem("sums_seeded")
        s_ones = sem("sums_row_of_ones")
        s_last = sem("last_sources_ready")
        s_lastw = sem("last_sources_written")
        s_bc = [[sem(f"src_broadcast{n}_{i}") for i in range(2)] for n in range(2)]
        s_off = [sem("src_offset0_ready"), sem("src_offset1_ready")]
        s_pick = [sem("pick0_ready"), sem("pick1_ready")]
        s_picked = [sem("picked0"), sem("picked1")]
        s_prow = [sem("picked_rows0_ready"), sem("picked_rows1_ready")]
        s_hi = [sem("high_part0"), sem("high_part1")]
        s_rest = [sem("rest_part0"), sem("rest_part1")]
        s_mid = [sem("middle_part0"), sem("middle_part1")]
        s_parts = [sem("parts0_ready"), sem("parts1_ready")]
        s_tab = sem("table1_multiplied")
        s_tabc = sem("table1_copied")
        s_idx = [sem(f"idx_ready{s}") for s in range(SLOTS)]
        s_gat = [sem(f"gathered{s}") for s in range(SLOTS)]
        s_ea = [sem(f"edge_attr_loaded{s}") for s in range(SLOTS)]
        s_dw = [sem("dw0_ready"), sem("dw1_ready")]
        s_oh = [sem("onehot0_ready"), sem("onehot1_ready")]
        s_win = [sem("window0_summed"), sem("window1_summed")]
        s_acc = [sem("window0_added"), sem("window1_added")]
        s_more_dw = [sem("more_dw0_ready"), sem("more_dw1_ready")]
        s_more_oh = [sem("more_onehot0_ready"), sem("more_onehot1_ready")]
        s_more_win = [sem("more_window0_summed"), sem("more_window1_summed")]
        s_more_acc = [sem("more_window0_added"), sem("more_window1_added")]
        s_done = sem("group1_summed")
        s_passed = sem("waits_passed")
        s_et = sem("edge_attr_transposed")
        s_etc = sem("edge_attr_T_copied")
        s_em = sem("edge_attr_multiplied")
        s_used = [sem(f"rows_used{s}") for s in range(SLOTS)]
        s_msg = sem("message_ready")
        s_fin_mm = sem("update_multiplied")
        s_fin_g = sem("update_gelu")
        s_fin = sem("update_added")
        s_out = sem("out_written")

        block = ctx.enter_context(nc.Block())

        def part(t, n):
            return t[:, n * PC:(n + 1) * PC, :]

        @block.sync
        def _(sp):
            for one in (*s_used, *s_prow):
                sp.sem_inc(one, 1)
            for one in (s_msg, s_done, *s_acc):
                sp.sem_inc(one, 2)
            sp.dma_start(x_sb[:, :, :], x_view).then_inc(s_x, 16)

            def load_edges(to, a, loaded):
                sp.dma_start(to[:, 0, :], a[0:P * G].rearrange("(r e) -> r e", e=G)).then_inc(loaded, 16)
                sp.dma_start(to[0:HALF[1] - 1, 1, :],
                             a[P * G:LAST * G].rearrange("(r e) -> r e", e=G)).then_inc(loaded, 16)
                sp.dma_start(to[HALF[1] - 1:HALF[1], 1, :],
                             a[E - G:E].rearrange("(r e) -> r e", e=G)).then_inc(loaded, 16)

            load_edges(src_raw, src, s_src)
            load_edges(dst_raw, dst, s_dst)
            load_edges(w_raw, edge_weight, s_wt)
            def load_bc(layer, q, i):
                v = last_src.rearrange("g e -> (g e)")[bass.ds(q * PE2, PE2)].rearrange("(a n) -> a n", a=1)
                sp.dma_start(src_bc[:, i, :], v.to_broadcast([PN, PE2])).then_inc(s_bc[layer][i], 16)

            for n in range(PARTS):
                sp.wait_ge(s_h[0], n + 1)
                sp.dma_start(part(h0_view, n), part(h_sb, n)).then_inc(s_tabw[0][n], 16)
            sp.wait_ge(s_last, 1)
            sp.dma_start(last_src[0:P, :], src_last[:, 0, :]).then_inc(s_lastw, 16)
            sp.dma_start(last_src[P:NG, :], src_last[0:HALF[1], 1, :]).then_inc(s_lastw, 16)
            sp.wait_ge(s_lastw, 32)
            for i in range(2):
                load_bc(0, i, i)
            sp.wait_ge(s_const, 6)
            sp.dma_start(W0_sb[0:D, 0:D], W0).then_inc(s_w, 16)
            sp.dma_start(W0_sb[D:DA, 0:D], b0.rearrange("(a n) -> a n", a=1)).then_inc(s_w, 16)
            sp.dma_start(W1a_sb[0:D, :], W_msg[0:D, :]).then_inc(s_w, 16)
            sp.dma_start(W1a_sb[D:DA, :], b_msg.rearrange("(a n) -> a n", a=1)).then_inc(s_w, 16)
            for h in range(2):
                sp.dma_start(W1b_sb[h * D:(h + 1) * D, h * D:(h + 1) * D], W_msg[D:2 * D, :]).then_inc(s_w, 16)
            sp.dma_start(Wu_sb[0:D, :], W_upd).then_inc(s_w, 16)
            sp.dma_start(Wu_sb[D:DA, :], b_upd.rearrange("(a n) -> a n", a=1)).then_inc(s_w, 16)
            sp.dma_start(eps_sb[:, :], eps.rearrange("(a n) -> a n", a=1).to_broadcast([D, 1])).then_inc(s_w, 16)

            def load_ea(g, s):
                at = E - G if isinstance(g, int) and g == LAST else g * G
                v = edge_attr[bass.ds(at, G), :].rearrange("(p j) d -> p (j d)", j=J)
                sp.dma_start(ea[:, s, :], v).then_inc(s_ea[s], 16)

            for s in range(SLOTS):
                load_ea(s, s)

            def next_bc(layer, b, s):
                sp.wait_ge(s_pick[layer], 2 * b + (s // 2 + 2))
                load_bc(layer, 2 * b + (s // 2 + 3), (s // 2 + 1) % 2)

            sp.wait_ge(s_pick[0], 1)
            load_bc(0, 2, 0)
            with sp.Fori(0, BODIES - 2) as b:
                for s in (0, 2):
                    next_bc(0, b, s)
            next_bc(0, BODIES - 2, 0)
            sp.wait_ge(s_pick[0], PAIRS)
            for i in range(2):
                load_bc(1, i, i)
            sp.wait_ge(s_pick[1], 1)
            load_bc(1, 2, 0)
            for n in range(PARTS):
                sp.wait_ge(s_tabc, PC * (n + 1))
                sp.dma_start(part(p1_view, n), part(h_sb, n)).then_inc(s_tabw[1][n], 16)
            with sp.Fori(0, BODIES - 2) as b:
                for s in range(SLOTS):
                    sp.wait_ge(s_et, b * SLOTS + (s + 1))
                    load_ea((b + 1) * SLOTS + s, s)
                    if s % 2 == 0:
                        next_bc(1, b, s)
            for s in range(SLOTS):
                sp.wait_ge(s_et, (BODIES - 2) * SLOTS + s + 1)
                load_ea((BODIES - 1) * SLOTS + s, s)
                if s == 0:
                    next_bc(1, BODIES - 2, 0)
            for c in range(0, NC, 2):
                sp.wait_ge(s_fin, c + 2)
                sp.dma_start(out_view[:, c:c + 2, :], h_sb[:, c:c + 2, :]).then_inc(s_out, 16)
            sp.wait_ge(s_out, NC // 2 * 16)

        @block.gpsimd
        def _(pool):
            nc.gpsimd.memset(ident[:, :], 0.0).then_inc(s_identf, 1)
            pool.wait_ge(s_identf, 1)
            nc.gpsimd.affine_select(out=ident[:, :], in_=ident[:, :], compare_op=ALU.not_equal, fill=1.0,
                                    base=0, pattern=[[-1, P]], channel_multiplier=1).then_inc(s_const, 1)
            nc.gpsimd.iota(iota_i[:, :], pattern=[[1, WIN]], base=0, channel_multiplier=0).then_inc(s_const, 1)
            nc.gpsimd.memset(rows[:, :, :, D:DA], 1.0).then_inc(s_const, 1)
            nc.gpsimd.iota(node_i[:, :], pattern=[[1, 1]], base=0,
                           channel_multiplier=KN).then_inc(s_const, 1)
            for layer, table in ((0, h0_table), (1, p1_table)):
                if layer == 1:
                    pool.wait_ge(s_agg, NC)
                    nc.gpsimd.memset(sums_sb[D:DA, :], 1.0).then_inc(s_ones, 1)
                for n in range(PARTS):
                    pool.wait_ge(s_tabw[layer][n], 16)
                with pool.Fori(layer * BODIES + 1, (layer + 1) * BODIES + 1) as turn:
                    for s in range(SLOTS):
                        pool.wait_ge(s_const, 6)
                        pool.wait_ge(s_idx[s], turn)
                        pool.wait_ge(s_used[s], turn)
                        for j in range(JG):
                            nc.gpsimd.indirect_dma_start(
                                out=rows[:, s, j, 0:D], out_offset=None, in_=table[:, :],
                                in_offset=bass.IndirectOffsetOnAxis(ap=idx[:, s, j:j + 1].bitcast(u32), axis=0),
                            ).then_inc(s_gat[s], 16)

        @block.scalar
        def _(act):
            def copy_idx(g, s):
                nc.scalar.copy(idx[:, s, :], src_tab[:, bass.ds(g * J, J)]).then_inc(s_idx[s], 1)

            def norm(layer):
                for n in range(PARTS):
                    act.wait_ge(s_sub[layer], n + 1)
                    if n:
                        act.wait_ge(s_var[layer], n)
                    nc.scalar.activation(sq[:, :, :], part(h_sb, n), ACT.Square).then_inc(s_sq[layer], 1)
                for n in range(PARTS):
                    at = slice(n * PC * KN, (n + 1) * PC * KN)
                    act.wait_ge(s_var[layer], n + 1)
                    nc.scalar.activation(ln_m[:, 3, at], ln_m[:, 2, at], ACT.Sqrt).then_inc(s_std[layer], 1)

            def split(layer, n):
                rows_n = h_sb[:, n * PC:(n + 1) * PC, :].rearrange("p c (k d) -> p (c k) d", d=D)
                to = parts[:, n * PC * KN:(n + 1) * PC * KN, :]
                nc.scalar.copy(to[:, :, 0:D], rows_n).then_inc(s_hi[layer], 1)
                act.wait_ge(s_rest[layer], n + 1)
                nc.scalar.copy(to[:, :, D:2 * D], sq[:, :, :].rearrange("p c (k d) -> p (c k) d", d=D)).then_inc(
                    s_mid[layer], 1)

            norm(0)
            act.wait_ge(s_src, 48)
            nc.scalar.copy(src_f[:, 0, :], src_raw[:, 0, :])
            nc.scalar.copy(src_f[0:HALF[1], 1, :], src_raw[0:HALF[1], 1, :]).then_inc(s_srcf, 1)
            nc.scalar.copy(src_last[:, 0, :], src_raw[:, 0, :].rearrange("r (p j) -> r j p", j=J)[:, JG, :])
            nc.scalar.copy(src_last[0:HALF[1], 1, :],
                           src_raw[0:HALF[1], 1, :].rearrange("r (p j) -> r j p", j=J)[:, JG, :]).then_inc(s_last, 1)
            act.wait_ge(s_dst, 48)
            nc.scalar.copy(dst_f[:, 0, :], dst_raw[:, 0, :])
            nc.scalar.copy(dst_f[0:HALF[1], 1, :], dst_raw[0:HALF[1], 1, :]).then_inc(s_dstf, 1)
            for half in range(2):
                r = HALF[half]
                act.wait_ge(s_tr, half + 1)
                for m in range(2):
                    last = nc.scalar.copy(
                        src_tab[:, :].rearrange("p (g j) -> p j g", j=J)[:, 4 * m:4 * m + 4, half * P:half * P + r],
                        psR[half % 2][:, m, :].rearrange("p (j g) -> p j g", g=P)[:, :, 0:r])
                last.then_inc(s_srct, 1)
            act.wait_ge(s_srct, 2)
            for s in range(SLOTS):
                copy_idx(s, s)
            for n in range(PARTS):
                act.wait_ge(s_h[0], n + 1)
                split(0, n)
            with act.Fori(0, BODIES - 1) as b:
                for s in range(SLOTS):
                    act.wait_ge(s_gat[s], (b + 1) * (16 * JG))
                    copy_idx((b + 1) * SLOTS + s, s)
            for s in range(SLOTS):
                act.wait_ge(s_gat[s], BODIES * 16 * JG)
                copy_idx(s, s)
            norm(1)
            for c in range(NC):
                act.wait_ge(s_ht, c + 1)
                if c >= 2:
                    act.wait_ge(s_tab, c - 1)
                    act.wait_ge(s_seed, c - 1)
                nc.scalar.copy(hT[0:D, c % 2, 0:4 * PN], psR[c % 2][0:D, 0, 0:4 * PN])
                nc.scalar.copy(hT[0:D, c % 2, 4 * PN:5 * PN], psR[c % 2][0:D, 1, 0:PN]).then_inc(s_htc, 1)
                act.wait_ge(s_tab, c + 1)
                nc.scalar.copy(h_sb[:, c, :], psN[c % 2][0:PN, 0:KN * D]).then_inc(s_tabc, 1)
            act.wait_ge(s_tabc, NC)
            act.wait_ge(s_picked[0], NG)
            for n in range(PARTS):
                split(1, n)

            def message(b, s):
                act.wait_ge(s_et, b * SLOTS + (s + 1))
                nc.scalar.copy(eT[:, :], psT[:, :]).then_inc(s_etc, 1)
                act.wait_ge(s_used[s], b + (1 + BODIES + 1))
                act.wait_ge(s_done, b * SLOTS + (s + 1))
                nc.scalar.activation(msg[:, s % 2, :], pre[:, s % 2, :], ACT.Gelu_apprx_tanh).then_inc(s_msg, 1)

            with act.Fori(0, BODIES - 1) as b:
                for s in range(SLOTS):
                    message(b, s)
                    copy_idx((b + 1) * SLOTS + s, s)
            for s in range(SLOTS):
                message(BODIES - 1, s)
            for c in range(NC):
                act.wait_ge(s_fin_mm, c + 1)
                nc.scalar.activation(h_sb[:, c, :], psN[c % 2][0:PN, 0:KN * D], ACT.Gelu_apprx_tanh).then_inc(s_fin_g, 1)

        @block.tensor
        def _(pe):
            pe.wait_ge(s_const, 6)

            def turn(a, half, to):
                r = HALF[half]
                v = a[0:r, half, :].rearrange("r (p j) -> r j p", j=J)
                for j in range(J):
                    last = nc.tensor.transpose(to[:, j // 4, (j % 4) * P:(j % 4) * P + r],
                                               v[:, j, :], ident[0:r, 0:r])
                last.then_inc(s_tr, 1)

            pe.wait_ge(s_srcf, 1)
            turn(src_f, 0, psR[0])
            turn(src_f, 1, psR[1])
            pe.wait_ge(s_stats, 1)
            for half in range(2):
                r = HALF[half]
                for q in range(2):
                    last = nc.tensor.transpose(psS[0:1, q * 256 + half * P:q * 256 + half * P + r],
                                               stat[0:r, half, q * 3:q * 3 + 1], ident[0:r, 0:r])
            last.then_inc(s_stat_t, 1)
            pe.wait_ge(s_dstf, 1)
            pe.wait_ge(s_srct, 1)
            turn(dst_f, 0, psR[0])
            pe.wait_ge(s_srct, 2)
            turn(dst_f, 1, psR[1])
            pe.wait_ge(s_rowf, 1)
            nc.tensor.matmul(psS[:, 0:NG], ones_row[:, :], row_f[:, 0, :],
                             start=True, stop=True).then_inc(s_base_ps, 1)
            pe.wait_ge(s_wt, 48)
            for half in range(2):
                pe.wait_ge(s_dwt, half + 1)
                turn(w_raw, half, psR[half])

            def gather(layer, b, s, shift):
                g = b * SLOTS + (s + shift)
                pair = 2 * b + (s + shift) // 2
                at = (s + shift) % 2 * P
                pe.wait_ge(s_pick[layer], pair + 1)
                if shift:
                    pe.wait_ge(s_prow[layer], g)
                for n in range(NK):
                    last = nc.tensor.matmul(psG[(s + shift) % 2], pick[0:PN, (s + shift) // 2 % 2, n, at:at + P], parts[:, n, :],
                                            start=(n == 0), stop=(n == NK - 1))
                last.then_inc(s_picked[layer], 1)

            def windows(layer, b, s, lhs, width):
                g = b * SLOTS + s
                pe.wait_ge(s_oh[layer], b * SLOTS + (s + 1))
                pe.wait_ge(s_acc[layer], b * SLOTS + (s + 1))

                def product(done):
                    for j in range(J):
                        last = nc.tensor.matmul(psW[s % 2][0:width, :], lhs(j), onehot[:, s % 2, j, :],
                                                start=(j == 0), stop=(j == J - 1))
                    last.then_inc(done[layer], 1)

                product(s_win)
                count = pe.value_load(row_i[0:1, bass.ds(g, 1), 1], min_val=1, max_val=MAXW)
                with pe.If(count > 1):
                    before = pe.value_load(row_i[0:1, bass.ds(g, 1), 2], min_val=0, max_val=MAXW * NG)
                    with pe.Fori(0, count - 1) as i:
                        pe.wait_ge(s_more_oh[layer], before + i + 1)
                        product(s_more_win)

            pe.wait_ge(s_tables, 1)
            pe.wait_ge(s_parts[0], PARTS)
            gather(0, 0, 0, 0)

            def first(b, last_body):
                for s in range(SLOTS):
                    if not (last_body and s == SLOTS - 1):
                        gather(0, b, s, 1)
                    pe.wait_ge(s_gat[s], (b + 1) * (16 * JG))
                    pe.wait_ge(s_prow[0], b * SLOTS + (s + 2))
                    windows(0, b, s, lambda j, s=s: rows[:, s, j, :], DA)

            with pe.Fori(0, BODIES - 1) as b:
                first(b, False)
            first(BODIES - 1, True)

            for s in range(SLOTS):
                pe.wait_ge(s_used[s], BODIES + 1)
            pe.wait_ge(s_acc[0], NG + 2)
            pe.wait_ge(s_w, 16 * 9)

            def sums_product(sums, c, W, width, done):
                v = sums[:, c * CHUNK:(c + 1) * CHUNK].rearrange("f (p k) -> f k p", k=KN)
                for k in range(KN):
                    last = nc.tensor.matmul(psN[c % 2][0:PN, k * width:(k + 1) * width], v[:, k, :], W,
                                            start=True, stop=True)
                last.then_inc(done, 1)

            for c in range(NC):
                if c >= 2:
                    pe.wait_ge(s_x1, c - 1)
                sums_product(sums_sb, c, W0_sb[:, :], DA, s_agg)
            for c in range(NC + 1):
                if c < NC:
                    pe.wait_ge(s_h[1], c // PC + 1)
                    if c >= 2:
                        pe.wait_ge(s_htc, c - 1)
                    for k in range(KN):
                        last = nc.tensor.transpose(psR[c % 2][0:D, k // 4, k % 4 * PN:(k % 4 + 1) * PN],
                                                   h_sb[:, c, k * D:(k + 1) * D], ident[0:PN, 0:PN])
                    last.then_inc(s_ht, 1)
                if c:
                    n = c - 1
                    pe.wait_ge(s_htc, n + 1)
                    if n >= 2:
                        pe.wait_ge(s_tabc, n - 1)
                    for k in range(KN):
                        last = nc.tensor.matmul(psN[n % 2][0:PN, k * D:(k + 1) * D],
                                                hT[:, n % 2, k * PN:(k + 1) * PN], W1a_sb[:, :],
                                                start=True, stop=True)
                    last.then_inc(s_tab, 1)

            def edge_transpose(b, s, shift):
                slot = (s + shift) % SLOTS
                g = b * SLOTS + (s + shift)
                pe.wait_ge(s_ea[slot], (b + (s + shift) // SLOTS + 1) * 16)
                if shift:
                    pe.wait_ge(s_etc, g)
                for q in range(J // 2):
                    last = nc.tensor.transpose(psT[:, q * P:(q + 1) * P], ea[:, slot, q * P:(q + 1) * P],
                                               ident[:, :])
                last.then_inc(s_et, 1)

            def edge_product(b, s, shift):
                g = b * SLOTS + (s + shift)
                pe.wait_ge(s_etc, g + 1)
                if shift:
                    pe.wait_ge(s_used[s], b + (1 + BODIES + 1))
                for q in range(J // 2):
                    last = nc.tensor.matmul(psM[:, q * P:(q + 1) * P], eT[:, q * P:(q + 1) * P],
                                            W1b_sb[:, :], start=True, stop=True)
                last.then_inc(s_em, 1)

            pe.wait_ge(s_tabc, NC)
            edge_transpose(0, 0, 0)
            pe.wait_ge(s_parts[1], PARTS)
            gather(1, 0, 0, 0)
            edge_product(0, 0, 0)

            def second(b, last_body):
                for s in range(SLOTS):
                    if not (last_body and s == SLOTS - 1):
                        edge_transpose(b, s, 1)
                        gather(1, b, s, 1)
                        edge_product(b, s, 1)
                    pe.wait_ge(s_msg, b * SLOTS + (s + 1 + 2))
                    windows(1, b, s, lambda j, s=s: msg[:, s % 2, j * D:(j + 1) * D], D)

            with pe.Fori(0, BODIES - 1) as b:
                second(b, False)
            second(BODIES - 1, True)

            pe.wait_ge(s_done, NG + 2)
            pe.wait_ge(s_ones, 1)
            pe.wait_ge(s_acc[1], NG + 2)
            for c in range(NC):
                if c >= 2:
                    pe.wait_ge(s_fin_g, c - 1)
                sums_product(sums_sb, c, Wu_sb[:, :], D, s_fin_mm)

        @block.vector
        def _(dve):
            at = [0, 0]

            def meta(ins):
                at[0] += 1
                ins.then_inc(s_dvm, 1)
                dve.wait_ge(s_dvm, at[0])

            def step(ins):
                at[1] += 1
                ins.then_inc(s_ln, 1)
                dve.wait_ge(s_ln, at[1])

            nc.vector.memset(W1b_sb[:, :], 0.0).then_inc(s_const, 1)
            step(nc.vector.memset(W0_sb[:, :], 0.0))
            nc.vector.memset(W0_sb[D:DA, D:DA], 1.0)
            nc.vector.memset(ones_row[:, :], 1.0).then_inc(s_const, 1)

            def k3(t):
                return t.rearrange("p c (k d) -> p (c k) d", d=D)

            def layer_norm(layer):
                def m(q, n):
                    return ln_m[:, q, n * PC * KN:(n + 1) * PC * KN]

                def mb(q, n):
                    return m(q, n).unsqueeze(2).to_broadcast([PN, PC * KN, D])

                for n in range(PARTS):
                    step(nc.vector.tensor_reduce(m(0, n), k3(part(x_sb, n)), AX.X, ALU.add))
                    step(nc.vector.tensor_scalar(m(1, n), m(0, n), 1.0 / D, None, ALU.mult))
                    nc.vector.tensor_tensor(k3(part(h_sb, n)), k3(part(x_sb, n)), mb(1, n),
                                            ALU.subtract).then_inc(s_sub[layer], 1)
                for n in range(PARTS):
                    dve.wait_ge(s_sq[layer], n + 1)
                    step(nc.vector.tensor_reduce(m(4, n), k3(sq[:, :, :]), AX.X, ALU.add))
                    nc.vector.tensor_scalar(m(2, n), m(4, n), 1.0 / D, LN_EPS,
                                            ALU.mult, ALU.add).then_inc(s_var[layer], 1)
                for n in range(PARTS):
                    dve.wait_ge(s_std[layer], n + 1)
                    step(nc.vector.reciprocal(m(5, n), m(3, n)))
                    nc.vector.scalar_tensor_tensor(out=k3(part(h_sb, n)), in0=k3(part(h_sb, n)), scalar=0.0,
                                                   in1=mb(5, n), op0=ALU.max, op1=ALU.mult).then_inc(s_h[layer], 1)

            dve.wait_ge(s_x, 16)
            layer_norm(0)

            dve.wait_ge(s_const, 6)
            meta(nc.vector.tensor_copy(iota[:, :], iota_i[:, :]))
            nc.vector.memset(sums_sb[:, :], 0.0).then_inc(s_zero, 1)
            meta(nc.vector.tensor_copy(node_f[:, :], node_i[:, :]))
            nc.vector.memset(hT[D:DA, :, :], 1.0)
            meta(nc.vector.memset(minus_row[:, :], -1.0))

            dve.wait_ge(s_dstf, 1)
            for half in range(2):
                r = HALF[half]
                nc.vector.tensor_reduce(stat[0:r, half, 0:1], dst_f[0:r, half, :], AX.X, ALU.min)
                meta(nc.vector.tensor_reduce(stat[0:r, half, 1:2], dst_f[0:r, half, :], AX.X, ALU.max))
                meta(nc.vector.tensor_tensor(stat[0:r, half, 2:3], stat[0:r, half, 1:2], stat[0:r, half, 0:1],
                                             ALU.subtract))
                meta(nc.vector.tensor_copy(stat_i[0:r, half, :], stat[0:r, half, 2:3]))
                meta(nc.vector.tensor_scalar(stat_i[0:r, half, :], stat_i[0:r, half, :], 7, None,
                                             ALU.logical_shift_right))
                last = nc.vector.tensor_scalar_add(stat[0:r, half, 3:4], stat_i[0:r, half, :], 1.0)
            last.then_inc(s_stats, 1)

            def take(first, to):
                for half in range(2):
                    r = HALF[half]
                    dve.wait_ge(s_tr, first + half + 1)
                    for m in range(2):
                        last = nc.vector.tensor_copy(
                            to[:, half * P:half * P + r, 4 * m:4 * m + 4].rearrange("p g j -> p j g"),
                            psR[half][:, m, :].rearrange("p (j g) -> p j g", g=P)[:, :, 0:r])
                    last.then_inc(s_dwt, 1)

            dve.wait_ge(s_stat_t, 1)
            meta(nc.vector.tensor_copy(row_f[:, 0:2, :],
                                       psS[0:1, :].rearrange("a (q g) -> a q g", q=2)[:, :, 0:NG]))
            nc.vector.tensor_tensor_scan(row_f[:, 2, :], row_f[:, 1, :], minus_row[:, :], 0.0,
                                         ALU.add, ALU.add).then_inc(s_rowf, 1)
            dve.wait_ge(s_rowf, 1)
            meta(nc.vector.scalar_tensor_tensor(out=row_f[:, 2, :], in0=row_f[:, 2, :], scalar=1.0,
                                                in1=row_f[:, 1, :], op0=ALU.add, op1=ALU.subtract))
            meta(nc.vector.tensor_copy(row_i[:, :, 0:3].rearrange("a g q -> a q g"), row_f[:, :, :]))
            take(2, dw_tab[:, :, 0, :])
            dve.wait_ge(s_base_ps, 1)
            meta(nc.vector.tensor_copy(base_bc[:, :], psS[:, 0:NG]))
            dve.wait_ge(s_dwt, 2)
            meta(nc.vector.tensor_tensor(dw_tab[:, :, 0, :], dw_tab[:, :, 0, :],
                                         base_bc[:, :].unsqueeze(2).to_broadcast([P, NG, J]), ALU.subtract))
            meta(nc.vector.memset(dw_tab[0:TWICE // J, LAST, 0, :], -1e6))
            take(4, dw_tab[:, :, 1, :])
            dve.wait_ge(s_dwt, 4)
            nc.vector.memset(tick[:, :], 0.0).then_inc(s_tables, 1)

            def onehots(layer, par, done):
                for j in range(J):
                    if layer == 0:
                        last = nc.vector.tensor_scalar(onehot[:, par, j, :], iota[:, :], dw[:, par, 0, j:j + 1],
                                                       dw[:, par, 1, j:j + 1], ALU.is_equal, ALU.mult)
                    else:
                        last = nc.vector.tensor_scalar(onehot[:, par, j, :], iota[:, :], dw[:, par, 0, j:j + 1],
                                                       None, ALU.is_equal)
                last.then_inc(done, 1)

            def first_onehots(layer, b, s, shift):
                g = b * SLOTS + (s + shift)
                par = (s + shift) % 2
                nc.vector.tensor_copy(dw[:, par, :, :], dw_tab[:, bass.ds(g, 1), :, :].rearrange(
                    "p a q j -> p (a q) j")).then_inc(s_dw[layer], 1)
                dve.wait_ge(s_dw[layer], b * SLOTS + (s + shift + 1))
                onehots(layer, par, s_oh[layer])

            def split(layer, n):
                rows_n = k3(part(h_sb, n))
                to = parts[:, n * PC * KN:(n + 1) * PC * KN, :]
                dve.wait_ge(s_hi[layer], n + 1)
                if n:
                    dve.wait_ge(s_parts[layer], n)
                nc.vector.tensor_tensor(k3(sq[:, :, :]), rows_n, to[:, :, 0:D], ALU.subtract).then_inc(s_rest[layer], 1)
                dve.wait_ge(s_mid[layer], n + 1)
                nc.vector.tensor_tensor(to[:, :, 2 * D:3 * D], k3(sq[:, :, :]), to[:, :, D:2 * D],
                                        ALU.subtract).then_inc(s_parts[layer], 1)

            def offsets(layer, i, loaded, q):
                dve.wait_ge(s_bc[layer][i], loaded)
                nc.vector.tensor_scalar(src_off[:, :], src_bc[:, i, :], node_f[:, 0:1], None,
                                        ALU.subtract).then_inc(s_off[layer], 1)
                dve.wait_ge(s_off[layer], q + 1)

            def pick_half(layer, i, half):
                for n in range(half * NK // 2, (half + 1) * NK // 2):
                    last = nc.vector.tensor_scalar(pick[0:PN, i, n, :], src_off[:, :],
                                                   float(n // KN * CHUNK + n % KN), None, ALU.is_equal)
                if half == 1:
                    last.then_inc(s_pick[layer], 1)

            def next_pick(layer, b, s):
                if s % 2:
                    dve.wait_ge(s_picked[layer], b * SLOTS + (s + 1))
                    offsets(layer, (s + 3) // 2 % 2, (b + (s + 3) // 4 + 1) * 16, 2 * b + (s + 3) // 2)
                    pick_half(layer, (s + 3) // 2 % 2, 0)
                else:
                    pick_half(layer, (s // 2 + 1) % 2, 1)

            def first_picks(layer):
                offsets(layer, 0, 16, 0)
                pick_half(layer, 0, 0)
                pick_half(layer, 0, 1)
                dve.wait_ge(s_pick[layer], 1)
                offsets(layer, 1, 16, 1)
                pick_half(layer, 1, 0)

            def picked_rows(layer, b, s, shift):
                slot = (s + shift) % SLOTS
                dve.wait_ge(s_picked[layer], b * SLOTS + (s + shift + 1))
                nc.vector.tensor_reduce(rows[:, slot, JG, 0:D], psG[slot % 2].rearrange("p (q d) -> p d q", q=SPLIT),
                                        AX.X, ALU.add).then_inc(s_prow[layer], 1)

            def windows_of(b, s):
                g = b * SLOTS + s
                base = dve.value_load(row_i[0:1, bass.ds(g, 1), 0], min_val=0, max_val=N - 1)
                count = dve.value_load(row_i[0:1, bass.ds(g, 1), 1], min_val=1, max_val=MAXW)
                return base, count

            def sums(layer, b, s, width, base, count):
                g = b * SLOTS + s
                par = s % 2
                dve.wait_ge(s_win[layer], b * SLOTS + (s + 1))
                dve.wait_ge(s_acc[layer], b * SLOTS + (s + 2))
                to = sums_sb[0:width, bass.ds(base, WIN)]
                nc.vector.tensor_tensor(to, to, psW[par][0:width, :], ALU.add).then_inc(s_acc[layer], 1)
                with dve.If(count > 1):
                    before = dve.value_load(row_i[0:1, bass.ds(g, 1), 2], min_val=0, max_val=MAXW * NG)
                    dve.wait_ge(s_acc[layer], b * SLOTS + (s + 3))
                    dve.sem_inc(s_passed, 1)
                    with dve.Fori(0, count - 1) as i:
                        k = before + i + 1
                        nc.vector.tensor_scalar_add(dw[:, par, 0, :], dw[:, par, 0, :],
                                                    -float(WIN)).then_inc(s_more_dw[layer], 1)
                        dve.wait_ge(s_more_dw[layer], k)
                        onehots(layer, par, s_more_oh[layer])
                        dve.wait_ge(s_more_win[layer], k)
                        at_node = nc.s_assert_within(base + i * WIN + WIN, 0, N - 1, skip_runtime_bounds_check_because=(
                            "a group has just enough windows to reach its greatest target, which is below N"))
                        to = sums_sb[0:width, bass.ds(at_node, WIN)]
                        nc.vector.tensor_tensor(to, to, psW[par][0:width, :], ALU.add).then_inc(s_more_acc[layer], 1)
                        dve.wait_ge(s_more_acc[layer], k)
                nc.vector.memset(tick[:, s:s + 1], 0.0).then_inc(s_used[s] if layer == 0 else s_done, 1)

            dve.wait_ge(s_zero, 1)
            for n in range(PARTS):
                split(0, n)
            first_picks(0)
            first_onehots(0, 0, 0, 0)
            picked_rows(0, 0, 0, 0)

            def first(b, last_body):
                for s in range(SLOTS):
                    if not (last_body and s == SLOTS - 1):
                        first_onehots(0, b, s, 1)
                    if not last_body or s == 0:
                        next_pick(0, b, s)
                    base, count = windows_of(b, s)
                    if not (last_body and s == SLOTS - 1):
                        picked_rows(0, b, s, 1)
                    sums(0, b, s, DA, base, count)

            with dve.Fori(0, BODIES - 1) as b:
                first(b, False)
            first(BODIES - 1, True)

            dve.wait_ge(s_picked[0], NG)
            first_picks(1)

            for c in range(NC):
                dve.wait_ge(s_agg, c + 1)
                agg = psN[c % 2][0:PN, 0:KN * DA].rearrange("p (k f) -> p k f", f=DA)
                xc = x_sb[:, c, :].rearrange("p (k d) -> p k d", d=D)
                hc = h_sb[:, c, :].rearrange("p (k d) -> p k d", d=D)
                step(nc.vector.tensor_scalar_add(deg[:, 0, :], agg[:, :, D], DEG_EPS))
                step(nc.vector.reciprocal(deg[:, 1, :], deg[:, 0, :]))
                step(nc.vector.tensor_tensor(hc, agg[:, :, 0:D],
                                             deg[:, 1, :].unsqueeze(2).to_broadcast([PN, KN, D]), ALU.mult))
                nc.vector.scalar_tensor_tensor(out=xc, in0=hc, scalar=0.0, in1=xc,
                                               op0=ALU.max, op1=ALU.add).then_inc(s_x1, 1)
            dve.wait_ge(s_x1, NC)
            layer_norm(1)
            step(nc.vector.tensor_scalar_add(scale1[:, :], eps_sb[:, :], 1.0))
            for c in range(NC):
                dve.wait_ge(s_htc, c + 1)
                v = sums_sb[0:D, c * CHUNK:(c + 1) * CHUNK].rearrange("f (p k) -> f k p", k=KN)
                nc.vector.tensor_scalar(v, hT[0:D, c % 2, :].rearrange("f (k p) -> f k p", k=KN),
                                        scale1[:, 0:1], None, ALU.mult).then_inc(s_seed, 1)
            dve.wait_ge(s_seed, NC)
            for n in range(PARTS):
                split(1, n)

            def message_sum(b, s, shift):
                slot = (s + shift) % SLOTS
                g = b * SLOTS + (s + shift)
                dve.wait_ge(s_em, g + 1)
                dve.wait_ge(s_gat[slot], BODIES * 16 * JG + (b + (s + shift) // SLOTS + 1) * (16 * JG))
                dve.wait_ge(s_prow[1], g + 2)
                dve.wait_ge(s_msg, g + 1)
                nc.vector.tensor_tensor(pre[:, slot % 2, :].rearrange("p (j d) -> p j d", d=D),
                                        psM.rearrange("p (j d) -> p j d", d=D), rows[:, slot, :, 0:D],
                                        ALU.add).then_inc(s_used[slot], 1)

            first_onehots(1, 0, 0, 0)
            picked_rows(1, 0, 0, 0)
            message_sum(0, 0, 0)

            def second(b, last_body):
                for s in range(SLOTS):
                    if not (last_body and s == SLOTS - 1):
                        first_onehots(1, b, s, 1)
                    if not last_body or s == 0:
                        next_pick(1, b, s)
                    base, count = windows_of(b, s)
                    if not (last_body and s == SLOTS - 1):
                        picked_rows(1, b, s, 1)
                        message_sum(b, s, 1)
                    sums(1, b, s, D, base, count)

            with dve.Fori(0, BODIES - 1) as b:
                second(b, False)
            second(BODIES - 1, True)

            for c in range(NC):
                dve.wait_ge(s_fin_g, c + 1)
                nc.vector.tensor_tensor(h_sb[:, c, :], h_sb[:, c, :], x_sb[:, c, :], ALU.add).then_inc(s_fin, 1)


_INS = ["x", "src", "dst", "edge_attr_64", "edge_weight", "L0_gnn_W", "L0_gnn_b", "L1_gnn_W_msg",
        "L1_gnn_b_msg", "L1_gnn_W_upd", "L1_gnn_b_upd", "L1_gnn_eps"]
_OUTS = [((6250, 64), "float32")]


def kernel(**inputs):
    import numpy as _np
    import concourse.bacc as _bacc
    from concourse import mybir as _mybir
    from concourse.bass_utils import run_bass_kernel_spmd as _run

    nc = _bacc.Bacc("TRN2", target_bir_lowering=False, num_devices=1)
    arrays, args = {}, []
    for name in _INS:
        a = _np.ascontiguousarray(inputs[name])
        arrays[f"in_{name}_dram"] = a
        args.append(nc.dram_tensor(f"in_{name}_dram", a.shape, _mybir.dt.from_np(a.dtype), kind="ExternalInput").ap())
    for i, (shape, dtype) in enumerate(_OUTS):
        dt = _mybir.dt.from_np(_np.dtype(dtype))
        args.append(nc.dram_tensor(f"out_{i}_dram", shape, dt, kind="ExternalOutput").ap())
    two_layer_gnn(nc, *args)
    r = _run(nc, [arrays], core_ids=[0])
    got = tuple(r.results[0][f"out_{i}_dram"] for i in range(len(_OUTS)))
    return got[0]
```

```python
import concourse.bass as bass
from concourse import mybir
from contextlib import ExitStack


def two_layer_gnn(
    nc: bass.Bass,
    x: bass.AP,
    src: bass.AP,
    dst: bass.AP,
    edge_attr: bass.AP,
    edge_weight: bass.AP,
    W0: bass.AP,
    b0: bass.AP,
    W_msg: bass.AP,
    b_msg: bass.AP,
    W_upd: bass.AP,
    b_upd: bass.AP,
    eps: bass.AP,
    out: bass.AP,
):
    fp32 = mybir.dt.float32
    i32 = mybir.dt.int32
    u16 = mybir.dt.uint16
    i16 = mybir.dt.int16
    bf16 = mybir.dt.bfloat16
    u32 = mybir.dt.uint32
    ALU = mybir.AluOpType
    ACT = mybir.ActivationFunctionType
    AX = mybir.AxisListType

    N, D = x.shape
    E = src.shape[0]
    P = 128

    PN = 125
    KN = 5
    CHUNK = PN * KN
    NC = N // CHUNK
    assert NC * CHUNK == N

    J = 8
    G = P * J
    SLOTS = 4
    NG = -(-E // G)
    NG = -(-NG // SLOTS) * SLOTS
    BODIES = NG // SLOTS
    LAST = NG - 1
    assert (NG - 1) * G < E <= NG * G
    TWICE = NG * G - E
    assert TWICE % J == 0
    WIN = 128
    MAXW = -(-N // WIN)
    DA = D + 1
    HALF = (P, NG - P)
    LN_EPS = 1e-5
    DEG_EPS = 1e-6

    NK = NC * KN

    JG = J - 1
    EXTRA = 2
    JP = [[JG - (layer == 0 and s == EXTRA) for s in range(SLOTS)] for layer in range(2)]
    SPLIT = 3
    PAIRS = NG // 2
    PE2 = 2 * P
    PE3 = 3 * P

    h0_table = nc.dram_tensor("h0_table", (N, D), fp32, kind="Internal").ap()
    p1_table = nc.dram_tensor("p1_table", (N, D), fp32, kind="Internal").ap()
    last_src = nc.dram_tensor("last_src", (2, NG, P), u16, kind="Internal").ap()

    x_view = x.rearrange("(c p k) d -> p c (k d)", p=PN, k=KN)
    out_view = out.rearrange("(c p k) d -> p c (k d)", p=PN, k=KN)
    h0_view = h0_table.rearrange("(c p k) d -> p c (k d)", p=PN, k=KN)
    p1_view = p1_table.rearrange("(c p k) d -> p c (k d)", p=PN, k=KN)

    UC = 2
    UNITS = NC // UC
    UN = UC * KN
    UQ = UN // 2
    UD = UN * D
    BANK = 512
    assert UC * UNITS == NC and UQ == 5
    CONSTS = 7

    ctx = ExitStack()
    with ctx:
        def sb(name, shape, dt=fp32):
            return ctx.enter_context(nc.sbuf_tensor(name, shape, dt))

        def sem(name):
            return ctx.enter_context(nc.semaphore(name))

        ident = sb("ident", [P, P])
        iota_i = sb("iota_i", [P, WIN], i32)
        iota = sb("iota", [P, WIN])
        ones_row = sb("ones_row", [1, P])
        W0_sb = sb("W0_sb", [DA, DA])
        W1a_sb = sb("W1a_sb", [P, P])
        bm_bc = sb("bm_bc", [PN, D])
        W1b_sb = sb("W1b_sb", [P, P])
        Wu_sb = sb("Wu_sb", [DA, D])
        eps_sb = sb("eps_sb", [P, 1])
        scale1 = sb("scale1", [P, 1])

        node_i = sb("node_i", [PN, 1], i32)
        node_f = sb("node_f", [PN, 1])
        parts = sb("parts", [PN, NK, SPLIT * D], bf16)
        src_bc = sb("src_bc", [PN, 2, PE3], u16)
        src_off = sb("src_off", [PN, PE3], i16)
        pick_all = sb("pick_all", [P, NK * (PE3 + PE2)], bf16)
        pick = [pick_all[:, 0:NK * PE3].rearrange("p (n e) -> p n e", n=NK),
                pick_all[:, NK * PE3:].rearrange("p (n e) -> p n e", n=NK)]

        flat_f = pick_all[:, :].bitcast(fp32)
        flat_i = pick_all[:, :].bitcast(i32)

        def prep(flat, n):
            return flat[:, n * 2 * G:(n + 1) * 2 * G].rearrange("p (h e) -> p h e", h=2)

        src_raw, dst_raw = prep(flat_i, 0), prep(flat_i, 1)
        src_f, dst_f, w_raw = prep(flat_f, 2), prep(flat_f, 3), prep(flat_f, 4)
        src_last = sb("src_last", [P, 2, 2, P], u16)
        src_tab = sb("src_tab", [P, NG * J], u16)
        dw_tab = sb("dw_tab", [P, NG, 2, J])
        stat = sb("stat", [P, 2, 4])
        stat_i = sb("stat_i", [P, 2, 1], i32)
        row_f = sb("row_f", [1, 3, NG])
        minus_row = sb("minus_row", [1, NG])
        row_i = sb("row_i", [1, NG, 4], i32)
        base_bc = sb("base_bc", [P, NG])

        x_sb = sb("x_sb", [PN, NC, KN * D])
        h_sb = sb("h_sb", [PN, NC, KN * D])
        sq = sb("sq", [PN, 2, UC, KN * D])
        ln_m = sb("ln_m", [PN, 4, NK])
        ln_eps = sb("ln_eps", [PN, 1])
        deg = sb("deg", [PN, 2, UC, KN])
        sums_sb = sb("sums_sb", [DA, N + WIN])

        idx = sb("idx", [P, SLOTS, J], i32)
        rows = sb("rows", [P, SLOTS, J, DA])
        ea = sb("ea", [P, SLOTS, J * D])
        eT = sb("eT", [P, J // 2 * P])
        room = sb("room", [P, 4 * J * D])
        pre = room[:, 0:2 * J * D].rearrange("p (i e) -> p i e", i=2)
        msg = room[:, 2 * J * D:].rearrange("p (i e) -> p i e", i=2)
        wrows = room[:, 0:2 * J * DA].rearrange("p (i j f) -> p i j f", i=2, j=J)
        hT = room[:, 0:2 * UQ * PN].rearrange("p (i e) -> p i e", i=2)
        dw = sb("dw", [P, SLOTS, 2, J])
        onehot = sb("onehot", [P, 2, J, WIN])
        tick = sb("tick", [1, SLOTS])

        ps = ctx.enter_context(nc.psum_tensor("ps", [P, 8, 512], fp32))
        psW = [ps[:, 0, 0:WIN], ps[:, 7, 0:WIN]]
        psT = ps[:, 1, :]
        psM = ps[:, 2, :]
        psR = [ps[:, 3:5, :], ps[:, 5:7, :]]
        psU = [ps[:, 1 + 2 * i:3 + 2 * i, :] for i in range(2)]
        psN = [ps[:, 1 + i, :] for i in range(2)]
        psH = ps[:, 5:7, :]
        psP = [ps[:, 0, :], ps[:, 7, :]]
        psS = ps[:, 7, :]
        psG = [ps[:, 3 + i, 0:SPLIT * D] for i in range(2)]
        psX = ps[:, 5, 0:SPLIT * D]

        s_w = sem("weights_loaded")
        s_x = [sem(f"x_loaded{u}") for u in range(UNITS)]
        s_src = sem("src_loaded")
        s_dst = sem("dst_loaded")
        s_wt = sem("edge_weight_loaded")
        s_const = sem("constants_ready")
        s_zero = sem("buffers_set")
        s_identf = sem("identity_step")
        s_dvm = sem("edge_table_step")
        s_srcf = sem("src_is_float")
        s_dstf = sem("dst_is_float")
        s_tr = sem("edge_array_transposed")
        s_srct = sem("src_table_part")
        s_dwt = sem("target_weight_table_part")
        s_stats = sem("group_stats_ready")
        s_stat_t = sem("group_stats_transposed")
        s_rowf = sem("base_row_ready")
        s_base_ps = sem("base_broadcast")
        s_tables = sem("edge_tables_ready")
        s_ln = sem("layer_norm_step")
        s_sub = [sem("centred0"), sem("centred1")]
        s_sq = [sem("squared0"), sem("squared1")]
        s_var = [sem("variance0_ready"), sem("variance1_ready")]
        s_std = [sem("std0_ready"), sem("std1_ready")]
        s_h = [sem("h0_ready"), sem("h1_ready")]
        s_tabw = [sem(f"table{n}_written") for n in range(2)]
        s_agg = sem("sums0_multiplied")
        s_x1 = sem("x1_ready")
        s_ht = sem("h1_transposed")
        s_htc = sem("h1_T_copied")
        s_seed = sem("sums_seeded")
        s_scale = sem("scale_ready")
        s_ones = sem("sums_row_of_ones")
        s_last = sem("last_sources_ready")
        s_lastw = sem("last_sources_written")
        s_bc = [[sem(f"src_broadcast{n}_{i}") for i in range(2)] for n in range(2)]
        s_off = [sem("src_offset0_ready"), sem("src_offset1_ready")]
        s_pick = [sem("pick0_ready"), sem("pick1_ready")]
        s_picked = [sem("picked0"), sem("picked1")]
        s_prow = [sem("picked_rows0_ready"), sem("picked_rows1_ready")]
        s_half = sem("pick0_half_ready")
        s_xused = sem("extra_half_picked")
        s_xpicked = sem("extra_picked")
        s_xrow = sem("extra_rows_ready")
        s_hi = [sem("high_part0"), sem("high_part1")]
        s_rest = [sem("rest_part0"), sem("rest_part1")]
        s_mid = [sem("middle_part0"), sem("middle_part1")]
        s_parts = [sem("parts0_ready"), sem("parts1_ready")]
        s_tab = sem("table1_multiplied")
        s_tabc = sem("table1_copied")
        s_idx = [sem(f"idx_ready{s}") for s in range(SLOTS)]
        s_gat = [sem(f"gathered{s}") for s in range(SLOTS)]
        s_ea = [sem(f"edge_attr_loaded{s}") for s in range(SLOTS)]
        s_dw = [sem("dw0_ready"), sem("dw1_ready")]
        s_oh = [sem("onehot0_ready"), sem("onehot1_ready")]
        s_win = [sem("window0_summed"), sem("window1_summed")]
        s_acc = [sem("window0_added"), sem("window1_added")]
        s_more_dw = [sem("more_dw0_ready"), sem("more_dw1_ready")]
        s_more_oh = [sem("more_onehot0_ready"), sem("more_onehot1_ready")]
        s_more_win = [sem("more_window0_summed"), sem("more_window1_summed")]
        s_more_acc = [sem("more_window0_added"), sem("more_window1_added")]
        s_done = sem("group1_summed")
        s_passed = sem("waits_passed")
        s_et = sem("edge_attr_transposed")
        s_etc = sem("edge_attr_T_copied")
        s_em = sem("edge_attr_multiplied")
        s_used = [sem(f"rows_used{s}") for s in range(SLOTS)]
        s_msg = sem("message_ready")
        s_fin_mm = sem("update_multiplied")
        s_fin_g = sem("update_gelu")
        s_fin = sem("update_added")
        s_out = sem("out_written")

        block = ctx.enter_context(nc.Block())

        def unit(t, u):
            return t[:, u * UC:(u + 1) * UC, :]

        def rows3(t):
            return t.rearrange("p c (k d) -> p (c k) d", d=D)

        def split_to(u):
            return parts[:, u * UN:(u + 1) * UN, :]

        def nodes_of(n):
            c, k = n // KN, n % KN
            return sums_sb[0:D, c * CHUNK:(c + 1) * CHUNK].rearrange("f (p k) -> f k p", k=KN)[:, k, :]

        @block.sync
        def _(sp):
            for one in (*s_used, *s_prow):
                sp.sem_inc(one, 1)
            for one in (s_msg, s_done, *s_acc):
                sp.sem_inc(one, 2)
            for u in range(UNITS):
                sp.dma_start(unit(x_sb, u), unit(x_view, u)).then_inc(s_x[u], 16)

            def load_edges(to, a, loaded):
                sp.dma_start(to[:, 0, :], a[0:P * G].rearrange("(r e) -> r e", e=G)).then_inc(loaded, 16)
                sp.dma_start(to[0:HALF[1] - 1, 1, :],
                             a[P * G:LAST * G].rearrange("(r e) -> r e", e=G)).then_inc(loaded, 16)
                sp.dma_start(to[HALF[1] - 1:HALF[1], 1, :],
                             a[E - G:E].rearrange("(r e) -> r e", e=G)).then_inc(loaded, 16)

            load_edges(src_raw, src, s_src)
            load_edges(dst_raw, dst, s_dst)
            load_edges(w_raw, edge_weight, s_wt)

            def load_bc(layer, q, i):
                v = last_src[1].rearrange("g e -> (g e)")[bass.ds(q * PE2, PE2)].rearrange("(a n) -> a n", a=1)
                sp.dma_start(src_bc[:, i, 0:PE2], v.to_broadcast([PN, PE2])).then_inc(s_bc[layer][i], 16)
                if layer == 0 and i == 0:
                    v = last_src[0].rearrange("g e -> (g e)")[bass.ds((q + EXTRA // 2) * PE2, P)].rearrange(
                        "(a n) -> a n", a=1)
                    sp.dma_start(src_bc[:, i, PE2:PE3], v.to_broadcast([PN, P])).then_inc(s_bc[layer][i], 16)

            for u in range(UNITS):
                sp.wait_ge(s_h[0], u + 1)
                sp.dma_start(unit(h0_view, u), unit(h_sb, u)).then_inc(s_tabw[0], 16)
            sp.wait_ge(s_last, 1)
            sp.dma_start(last_src[:, 0:P, :].rearrange("t g e -> g t e"), src_last[:, 0, :, :]).then_inc(s_lastw, 16)
            sp.dma_start(last_src[:, P:NG, :].rearrange("t g e -> g t e"),
                         src_last[0:HALF[1], 1, :, :]).then_inc(s_lastw, 16)
            sp.wait_ge(s_lastw, 32)
            for i in range(2):
                load_bc(0, i, i)
            sp.wait_ge(s_const, CONSTS)
            sp.dma_start(W0_sb[0:D, 0:D], W0).then_inc(s_w, 16)
            sp.dma_start(W0_sb[D:DA, 0:D], b0.rearrange("(a n) -> a n", a=1)).then_inc(s_w, 16)
            sp.dma_start(bm_bc[:, :], b_msg.rearrange("(a n) -> a n", a=1).to_broadcast([PN, D])).then_inc(s_w, 16)
            for h in range(2):
                sp.dma_start(W1a_sb[h * D:(h + 1) * D, h * D:(h + 1) * D], W_msg[0:D, :]).then_inc(s_w, 16)
                sp.dma_start(W1b_sb[h * D:(h + 1) * D, h * D:(h + 1) * D], W_msg[D:2 * D, :]).then_inc(s_w, 16)
            sp.dma_start(Wu_sb[0:D, :], W_upd).then_inc(s_w, 16)
            sp.dma_start(Wu_sb[D:DA, :], b_upd.rearrange("(a n) -> a n", a=1)).then_inc(s_w, 16)
            sp.dma_start(eps_sb[:, :], eps.rearrange("(a n) -> a n", a=1).to_broadcast([P, 1])).then_inc(s_w, 16)

            def load_ea(g, s):
                at = E - G if isinstance(g, int) and g == LAST else g * G
                v = edge_attr[bass.ds(at, G), :].rearrange("(p j) d -> p (j d)", j=J)
                sp.dma_start(ea[:, s, :], v).then_inc(s_ea[s], 16)

            for s in range(SLOTS):
                load_ea(s, s)

            def next_bc(layer, b, s):
                sp.wait_ge(s_pick[layer], 2 * b + (s // 2 + 2))
                load_bc(layer, 2 * b + (s // 2 + 3), (s // 2 + 1) % 2)

            sp.wait_ge(s_pick[0], 1)
            load_bc(0, 2, 0)
            with sp.Fori(0, BODIES - 2) as b:
                for s in (0, 2):
                    next_bc(0, b, s)
            next_bc(0, BODIES - 2, 0)
            sp.wait_ge(s_pick[0], PAIRS)
            for i in range(2):
                load_bc(1, i, i)
            sp.wait_ge(s_pick[1], 1)
            load_bc(1, 2, 0)
            for u in range(UNITS):
                sp.wait_ge(s_tabc, u + 1)
                sp.dma_start(unit(p1_view, u), unit(h_sb, u)).then_inc(s_tabw[1], 16)
            with sp.Fori(0, BODIES - 2) as b:
                for s in range(SLOTS):
                    sp.wait_ge(s_et, b * SLOTS + (s + 1))
                    load_ea((b + 1) * SLOTS + s, s)
                    if s % 2 == 0:
                        next_bc(1, b, s)
            for s in range(SLOTS):
                sp.wait_ge(s_et, (BODIES - 2) * SLOTS + s + 1)
                load_ea((BODIES - 1) * SLOTS + s, s)
                if s == 0:
                    next_bc(1, BODIES - 2, 0)
            for c in range(0, NC, 2):
                sp.wait_ge(s_fin, c + 2)
                sp.dma_start(out_view[:, c:c + 2, :], h_sb[:, c:c + 2, :]).then_inc(s_out, 16)
            sp.wait_ge(s_out, NC // 2 * 16)

        @block.gpsimd
        def _(pool):
            nc.gpsimd.memset(ident[:, :], 0.0).then_inc(s_identf, 1)
            pool.wait_ge(s_identf, 1)
            nc.gpsimd.affine_select(out=ident[:, :], in_=ident[:, :], compare_op=ALU.not_equal, fill=1.0,
                                    base=0, pattern=[[-1, P]], channel_multiplier=1).then_inc(s_const, 1)
            nc.gpsimd.iota(iota_i[:, :], pattern=[[1, WIN]], base=0, channel_multiplier=0).then_inc(s_const, 1)
            nc.gpsimd.memset(rows[:, :, :, D:DA], 1.0).then_inc(s_const, 1)
            nc.gpsimd.iota(node_i[:, :], pattern=[[1, 1]], base=0,
                           channel_multiplier=KN).then_inc(s_const, 1)
            nc.gpsimd.memset(sums_sb[:, :], 0.0).then_inc(s_zero, 1)
            pool.wait_ge(s_src, 48)
            nc.gpsimd.tensor_copy(src_f[:, 0, :], src_raw[:, 0, :])
            nc.gpsimd.tensor_copy(src_f[0:HALF[1], 1, :], src_raw[0:HALF[1], 1, :]).then_inc(s_srcf, 1)
            pool.wait_ge(s_dst, 48)
            nc.gpsimd.tensor_copy(dst_f[:, 0, :], dst_raw[:, 0, :])
            nc.gpsimd.tensor_copy(dst_f[0:HALF[1], 1, :], dst_raw[0:HALF[1], 1, :]).then_inc(s_dstf, 1)
            for layer, table in ((0, h0_table), (1, p1_table)):
                if layer == 1:
                    pool.wait_ge(s_agg, UNITS)
                    nc.gpsimd.memset(sums_sb[D:DA, :], 1.0).then_inc(s_ones, 1)
                pool.wait_ge(s_tabw[layer], UNITS * 16)
                with pool.Fori(layer * BODIES + 1, (layer + 1) * BODIES + 1) as turn:
                    for s in range(SLOTS):
                        pool.wait_ge(s_const, CONSTS)
                        pool.wait_ge(s_idx[s], turn)
                        pool.wait_ge(s_used[s], turn)
                        for j in range(JP[layer][s]):
                            nc.gpsimd.indirect_dma_start(
                                out=rows[:, s, j, 0:D], out_offset=None, in_=table[:, :],
                                in_offset=bass.IndirectOffsetOnAxis(ap=idx[:, s, j:j + 1].bitcast(u32), axis=0),
                            ).then_inc(s_gat[s], 16)

        @block.scalar
        def _(act):
            def copy_dw(layer, g, slot):
                nc.scalar.copy(dw[:, slot, :, :].rearrange("p q j -> p (q j)"),
                               dw_tab[:, bass.ds(g, 1), :, :].rearrange("p a q j -> p (a q j)")).then_inc(s_dw[layer], 1)

            def copy_idx(g, s):
                nc.scalar.copy(idx[:, s, :], src_tab[:, bass.ds(g * J, J)]).then_inc(s_idx[s], 1)

            def square(layer, u):
                act.wait_ge(s_sub[layer], u + 1)
                if u >= 2:
                    act.wait_ge(s_var[layer], u - 1)
                nc.scalar.activation(sq[:, u % 2, :, :], unit(h_sb, u), ACT.Square).then_inc(s_sq[layer], 1)

            def root(layer, u):
                at = slice(u * UN, (u + 1) * UN)
                act.wait_ge(s_var[layer], u + 1)
                nc.scalar.activation(ln_m[:, 2, at], ln_m[:, 1, at], ACT.Sqrt, bias=ln_eps[:, 0:1],
                                     scale=1.0 / D).then_inc(s_std[layer], 1)

            def high(layer, u):
                nc.scalar.copy(split_to(u)[:, :, 0:D], rows3(unit(h_sb, u))).then_inc(s_hi[layer], 1)

            def middle(layer, u):
                act.wait_ge(s_rest[layer], u + 1)
                nc.scalar.copy(split_to(u)[:, :, D:2 * D], rows3(sq[:, u % 2, :, :])).then_inc(s_mid[layer], 1)

            def take(first, to, done):
                for half in range(2):
                    r = HALF[half]
                    act.wait_ge(s_tr, first + half + 1)
                    for m in range(2):
                        last = nc.scalar.copy(
                            to[:, 4 * m:4 * m + 4, half * P:half * P + r],
                            psR[half][:, m, :].rearrange("p (j g) -> p j g", g=P)[:, :, 0:r])
                    last.then_inc(done, 1)

            for u in range(UNITS + 1):
                if u < UNITS:
                    square(0, u)
                if u:
                    root(0, u - 1)
            act.wait_ge(s_src, 48)
            nc.scalar.copy(src_last[:, 0, :, :], src_raw[:, 0, :].rearrange("r (p j) -> r j p", j=J)[:, JG - 1:J, :])
            nc.scalar.copy(src_last[0:HALF[1], 1, :, :],
                           src_raw[0:HALF[1], 1, :].rearrange("r (p j) -> r j p", j=J)[:, JG - 1:J, :]).then_inc(s_last, 1)
            take(0, src_tab[:, :].rearrange("p (g j) -> p j g", j=J), s_srct)
            act.wait_ge(s_srct, 2)
            for s in range(SLOTS):
                copy_idx(s, s)
            act.wait_ge(s_h[0], UNITS)
            for u in range(UNITS):
                high(0, u)
            take(2, dw_tab[:, :, 0, :].rearrange("p g j -> p j g"), s_dwt)
            for u in range(UNITS):
                middle(0, u)
            take(4, dw_tab[:, :, 1, :].rearrange("p g j -> p j g"), s_dwt)
            act.wait_ge(s_tables, 1)
            act.wait_ge(s_dwt, 4)
            for s in range(2):
                copy_dw(0, s, s)

            def first(b, last_body):
                for s in range(SLOTS):
                    g = b * SLOTS + s
                    act.wait_ge(s_gat[s], (b + 1) * (16 * JP[0][s]))
                    if last_body:
                        copy_idx(s, s)
                    else:
                        copy_idx((b + 1) * SLOTS + s, s)
                    act.wait_ge(s_done, g + 1)
                    if last_body and s >= 2:
                        copy_dw(1, s - 2, s - 2)
                    else:
                        copy_dw(0, g + 2, (s + 2) % SLOTS)
                    act.wait_ge(s_dw[0], g + 1)
                    act.wait_ge(s_prow[0], g + 2)
                    if s == EXTRA:
                        act.wait_ge(s_xrow, b + 1)
                    for j in range(J):
                        last = nc.scalar.activation(wrows[:, s % 2, j, :], rows[:, s, j, :], ACT.Copy,
                                                    scale=dw[:, s, 1, j:j + 1])
                    last.then_inc(s_used[s], 1)

            with act.Fori(0, BODIES - 1) as b:
                first(b, False)
            first(BODIES - 1, True)
            act.wait_ge(s_scale, 1)
            for u in range(UNITS + 2):
                if u >= 2:
                    v = u - 2
                    act.wait_ge(s_ht, v + 1)
                    if v >= 2:
                        act.wait_ge(s_tab, v - 1)
                    nc.scalar.copy(hT[:, v % 2, 0:4 * PN], psH[:, 0, 0:4 * PN])
                    nc.scalar.copy(hT[:, v % 2, 4 * PN:5 * PN], psH[:, 1, 0:PN]).then_inc(s_htc, 1)
                if u < UNITS:
                    square(1, u)
                if 1 <= u <= UNITS:
                    root(1, u - 1)
                if u >= 2:
                    act.wait_ge(s_htc, v + 1)
                    for n in range(UN):
                        last = nc.scalar.activation(
                            nodes_of(v * UN + n), hT[n % 2 * D:(n % 2 + 1) * D, v % 2, n // 2 * PN:(n // 2 + 1) * PN],
                            ACT.Copy, scale=scale1[n % 2 * D:(n % 2 + 1) * D, 0:1])
                    last.then_inc(s_seed, 1)
            act.wait_ge(s_picked[0], NG)
            for u in range(UNITS):
                act.wait_ge(s_tabc, u + 1)
                high(1, u)
                if u:
                    middle(1, u - 1)
            middle(1, UNITS - 1)

            def message(b, s):
                act.wait_ge(s_et, b * SLOTS + (s + 1))
                nc.scalar.copy(eT[:, :], psT[:, :]).then_inc(s_etc, 1)
                act.wait_ge(s_used[s], b + (1 + BODIES + 1))
                act.wait_ge(s_done, b * SLOTS + (NG + s + 1))
                nc.scalar.activation(msg[:, s % 2, :], pre[:, s % 2, :], ACT.Gelu_apprx_tanh).then_inc(s_msg, 1)

            with act.Fori(0, BODIES - 1) as b:
                for s in range(SLOTS):
                    message(b, s)
                    copy_dw(1, b * SLOTS + (s + 2), (s + 2) % SLOTS)
                    copy_idx((b + 1) * SLOTS + s, s)
            for s in range(SLOTS):
                message(BODIES - 1, s)
                if s < 2:
                    copy_dw(1, NG - SLOTS + s + 2, s + 2)
            for c in range(NC):
                act.wait_ge(s_fin_mm, c + 1)
                nc.scalar.activation(h_sb[:, c, :], psN[c % 2][0:PN, 0:KN * D], ACT.Gelu_apprx_tanh).then_inc(s_fin_g, 1)

        @block.tensor
        def _(pe):
            pe.wait_ge(s_const, CONSTS)

            def turn(a, half, to):
                r = HALF[half]
                v = a[0:r, half, :].rearrange("r (p j) -> r j p", j=J)
                for j in range(J):
                    last = nc.tensor.transpose(to[:, j // 4, (j % 4) * P:(j % 4) * P + r],
                                               v[:, j, :], ident[0:r, 0:r])
                last.then_inc(s_tr, 1)

            pe.wait_ge(s_srcf, 1)
            turn(src_f, 0, psR[0])
            turn(src_f, 1, psR[1])
            pe.wait_ge(s_stats, 1)
            for half in range(2):
                r = HALF[half]
                for q in range(2):
                    last = nc.tensor.transpose(psS[0:1, q * 256 + half * P:q * 256 + half * P + r],
                                               stat[0:r, half, q * 3:q * 3 + 1], ident[0:r, 0:r])
            last.then_inc(s_stat_t, 1)
            pe.wait_ge(s_dstf, 1)
            pe.wait_ge(s_srct, 1)
            turn(dst_f, 0, psR[0])
            pe.wait_ge(s_srct, 2)
            turn(dst_f, 1, psR[1])
            pe.wait_ge(s_rowf, 1)
            nc.tensor.matmul(psS[:, 0:NG], ones_row[:, :], row_f[:, 0, :],
                             start=True, stop=True).then_inc(s_base_ps, 1)
            pe.wait_ge(s_wt, 48)
            for half in range(2):
                pe.wait_ge(s_dwt, half + 1)
                turn(w_raw, half, psR[half])

            def gather(layer, b, s, shift):
                g = b * SLOTS + (s + shift)
                pair = 2 * b + (s + shift) // 2
                at = (s + shift) % 2 * P
                pe.wait_ge(s_pick[layer], pair + 1)
                if shift:
                    pe.wait_ge(s_prow[layer], g)
                for n in range(NK):
                    last = nc.tensor.matmul(psG[(s + shift) % 2], pick[(s + shift) // 2 % 2][0:PN, n, at:at + P],
                                            parts[:, n, :], start=(n == 0), stop=(n == NK - 1))
                last.then_inc(s_picked[layer], 1)

            def extra(q):
                for n in range(q * NK // 4, (q + 1) * NK // 4):
                    last = nc.tensor.matmul(psX, pick[0][0:PN, n, PE2:PE3], parts[:, n, :],
                                            start=(n == 0), stop=(n == NK - 1))
                return last

            def next_extra(b, s, last_body):
                if s == 0:
                    extra(2)
                elif s == 1:
                    extra(3).then_inc(s_xpicked, 1)
                elif s == 2 and not last_body:
                    pe.wait_ge(s_half, b + 1)
                    pe.wait_ge(s_xrow, b + 1)
                    extra(0)
                elif s == 3 and not last_body:
                    extra(1).then_inc(s_xused, 1)

            def windows(layer, b, s, lhs, width):
                g = b * SLOTS + s
                pe.wait_ge(s_oh[layer], b * SLOTS + (s + 1))
                pe.wait_ge(s_acc[layer], b * SLOTS + (s + 1))

                def product(done):
                    for j in range(J):
                        last = nc.tensor.matmul(psW[s % 2][0:width, :], lhs(j), onehot[:, s % 2, j, :],
                                                start=(j == 0), stop=(j == J - 1))
                    last.then_inc(done[layer], 1)

                product(s_win)
                count = pe.value_load(row_i[0:1, bass.ds(g, 1), 1], min_val=1, max_val=MAXW)
                with pe.If(count > 1):
                    before = pe.value_load(row_i[0:1, bass.ds(g, 1), 2], min_val=0, max_val=MAXW * NG)
                    with pe.Fori(0, count - 1) as i:
                        pe.wait_ge(s_more_oh[layer], before + i + 1)
                        product(s_more_win)

            pe.wait_ge(s_parts[0], UNITS)
            pe.wait_ge(s_dwt, 4)
            gather(0, 0, 0, 0)
            extra(0)
            extra(1).then_inc(s_xused, 1)
            pe.wait_ge(s_tables, 1)

            def first(b, last_body):
                for s in range(SLOTS):
                    if not (last_body and s == SLOTS - 1):
                        gather(0, b, s, 1)
                    next_extra(b, s, last_body)
                    pe.wait_ge(s_used[s], b + 2)
                    windows(0, b, s, lambda j, s=s: wrows[:, s % 2, j, :], DA)

            with pe.Fori(0, BODIES - 1) as b:
                first(b, False)
            first(BODIES - 1, True)

            pe.wait_ge(s_done, NG + 2)
            pe.wait_ge(s_acc[0], NG + 2)
            pe.wait_ge(s_w, 16 * 10)

            def sums_product(sums, c, W, width, to):
                v = sums[:, c * CHUNK:(c + 1) * CHUNK].rearrange("f (p k) -> f k p", k=KN)
                for k in range(KN):
                    last = nc.tensor.matmul(to[0:PN, k * width:(k + 1) * width], v[:, k, :], W,
                                            start=True, stop=True)
                return last

            for u in range(UNITS + 2):
                if u < UNITS:
                    if u >= 2:
                        pe.wait_ge(s_x1, u - 1)
                    for i in range(UC):
                        last = sums_product(sums_sb, u * UC + i, W0_sb[:, :], DA, psU[u % 2][:, i, :])
                    last.then_inc(s_agg, 1)
                if u >= 2:
                    v = u - 2
                    pe.wait_ge(s_h[1], v + 1)
                    if v:
                        pe.wait_ge(s_htc, v)
                    flat = unit(h_sb, v).rearrange("p c e -> p (c e)")
                    for q in range(UQ):
                        last = nc.tensor.transpose(psH[:, q // 4, q % 4 * PN:(q % 4 + 1) * PN],
                                                   flat[:, q * P:(q + 1) * P], ident[0:PN, 0:PN])
                    last.then_inc(s_ht, 1)
                    pe.wait_ge(s_htc, v + 1)
                    if v:
                        pe.wait_ge(s_tabc, v)
                    for q in range(UQ):
                        last = nc.tensor.matmul(psP[q // 4][0:PN, q % 4 * P:(q % 4 + 1) * P],
                                                hT[:, v % 2, q * PN:(q + 1) * PN], W1a_sb[:, :],
                                                start=True, stop=True)
                    last.then_inc(s_tab, 1)

            def edge_transpose(b, s, shift):
                slot = (s + shift) % SLOTS
                g = b * SLOTS + (s + shift)
                pe.wait_ge(s_ea[slot], (b + (s + shift) // SLOTS + 1) * 16)
                if shift:
                    pe.wait_ge(s_etc, g)
                for q in range(J // 2):
                    last = nc.tensor.transpose(psT[:, q * P:(q + 1) * P], ea[:, slot, q * P:(q + 1) * P],
                                               ident[:, :])
                last.then_inc(s_et, 1)

            def edge_product(b, s, shift):
                g = b * SLOTS + (s + shift)
                pe.wait_ge(s_etc, g + 1)
                if shift:
                    pe.wait_ge(s_used[s], b + (1 + BODIES + 1))
                for q in range(J // 2):
                    last = nc.tensor.matmul(psM[:, q * P:(q + 1) * P], eT[:, q * P:(q + 1) * P],
                                            W1b_sb[:, :], start=True, stop=True)
                last.then_inc(s_em, 1)

            pe.wait_ge(s_tabc, UNITS)
            edge_transpose(0, 0, 0)
            pe.wait_ge(s_parts[1], UNITS)
            gather(1, 0, 0, 0)
            edge_product(0, 0, 0)

            def second(b, last_body):
                for s in range(SLOTS):
                    if not (last_body and s == SLOTS - 1):
                        edge_transpose(b, s, 1)
                        gather(1, b, s, 1)
                        edge_product(b, s, 1)
                    pe.wait_ge(s_msg, b * SLOTS + (s + 1 + 2))
                    windows(1, b, s, lambda j, s=s: msg[:, s % 2, j * D:(j + 1) * D], D)

            with pe.Fori(0, BODIES - 1) as b:
                second(b, False)
            second(BODIES - 1, True)

            pe.wait_ge(s_done, 2 * NG + 2)
            pe.wait_ge(s_ones, 1)
            pe.wait_ge(s_acc[1], NG + 2)
            for c in range(NC):
                if c >= 2:
                    pe.wait_ge(s_fin_g, c - 1)
                sums_product(sums_sb, c, Wu_sb[:, :], D, psN[c % 2]).then_inc(s_fin_mm, 1)

        @block.vector
        def _(dve):
            at = [0, 0]

            def meta(ins):
                at[0] += 1
                ins.then_inc(s_dvm, 1)
                dve.wait_ge(s_dvm, at[0])

            def step(ins):
                at[1] += 1
                ins.then_inc(s_ln, 1)
                dve.wait_ge(s_ln, at[1])

            nc.vector.memset(W1b_sb[:, :], 0.0).then_inc(s_const, 1)
            step(nc.vector.memset(ln_eps[:, :], LN_EPS))
            nc.vector.memset(W1a_sb[:, :], 0.0).then_inc(s_const, 1)
            step(nc.vector.memset(W0_sb[:, :], 0.0))
            nc.vector.memset(W0_sb[D:DA, D:DA], 1.0)
            nc.vector.memset(ones_row[:, :], 1.0).then_inc(s_const, 1)

            def m(q, u):
                return ln_m[:, q, u * UN:(u + 1) * UN]

            def mb(q, u):
                return m(q, u).unsqueeze(2).to_broadcast([PN, UN, D])

            def centre(layer, u):
                step(nc.vector.tensor_reduce(m(0, u), rows3(unit(x_sb, u)), AX.X, ALU.add))
                nc.vector.scalar_tensor_tensor(out=rows3(unit(h_sb, u)), in0=mb(0, u), scalar=-1.0 / D,
                                               in1=rows3(unit(x_sb, u)), op0=ALU.mult,
                                               op1=ALU.add).then_inc(s_sub[layer], 1)

            def variance(layer, u):
                dve.wait_ge(s_sq[layer], u + 1)
                nc.vector.tensor_reduce(m(1, u), rows3(sq[:, u % 2, :, :]), AX.X, ALU.add).then_inc(s_var[layer], 1)

            def normed(layer, u):
                dve.wait_ge(s_std[layer], u + 1)
                step(nc.vector.reciprocal(m(3, u), m(2, u)))
                nc.vector.scalar_tensor_tensor(out=rows3(unit(h_sb, u)), in0=rows3(unit(h_sb, u)), scalar=0.0,
                                               in1=mb(3, u), op0=ALU.max, op1=ALU.mult).then_inc(s_h[layer], 1)

            def rest(layer, u):
                dve.wait_ge(s_hi[layer], u + 1)
                if u >= 2:
                    dve.wait_ge(s_parts[layer], u - 1)
                nc.vector.tensor_tensor(rows3(sq[:, u % 2, :, :]), rows3(unit(h_sb, u)), split_to(u)[:, :, 0:D],
                                        ALU.subtract).then_inc(s_rest[layer], 1)

            def low(layer, u):
                dve.wait_ge(s_mid[layer], u + 1)
                nc.vector.tensor_tensor(split_to(u)[:, :, 2 * D:3 * D], rows3(sq[:, u % 2, :, :]),
                                        split_to(u)[:, :, D:2 * D], ALU.subtract).then_inc(s_parts[layer], 1)

            for u in range(UNITS + 2):
                if u < UNITS:
                    dve.wait_ge(s_x[u], 16)
                    centre(0, u)
                if u >= 2:
                    normed(0, u - 2)
                if 1 <= u <= UNITS:
                    variance(0, u - 1)

            dve.wait_ge(s_const, CONSTS)
            meta(nc.vector.tensor_copy(iota[:, :], iota_i[:, :]))
            meta(nc.vector.tensor_copy(node_f[:, :], node_i[:, :]))
            meta(nc.vector.memset(minus_row[:, :], -1.0))

            dve.wait_ge(s_dstf, 1)
            for half in range(2):
                r = HALF[half]
                nc.vector.tensor_reduce(stat[0:r, half, 0:1], dst_f[0:r, half, :], AX.X, ALU.min)
                meta(nc.vector.tensor_reduce(stat[0:r, half, 1:2], dst_f[0:r, half, :], AX.X, ALU.max))
                meta(nc.vector.tensor_tensor(stat[0:r, half, 2:3], stat[0:r, half, 1:2], stat[0:r, half, 0:1],
                                             ALU.subtract))
                meta(nc.vector.tensor_copy(stat_i[0:r, half, :], stat[0:r, half, 2:3]))
                meta(nc.vector.tensor_scalar(stat_i[0:r, half, :], stat_i[0:r, half, :], 7, None,
                                             ALU.logical_shift_right))
                last = nc.vector.tensor_scalar_add(stat[0:r, half, 3:4], stat_i[0:r, half, :], 1.0)
            last.then_inc(s_stats, 1)

            dve.wait_ge(s_stat_t, 1)
            meta(nc.vector.tensor_copy(row_f[:, 0:2, :],
                                       psS[0:1, :].rearrange("a (q g) -> a q g", q=2)[:, :, 0:NG]))
            nc.vector.tensor_tensor_scan(row_f[:, 2, :], row_f[:, 1, :], minus_row[:, :], 0.0,
                                         ALU.add, ALU.add).then_inc(s_rowf, 1)
            dve.wait_ge(s_rowf, 1)
            meta(nc.vector.scalar_tensor_tensor(out=row_f[:, 2, :], in0=row_f[:, 2, :], scalar=1.0,
                                                in1=row_f[:, 1, :], op0=ALU.add, op1=ALU.subtract))
            meta(nc.vector.tensor_copy(row_i[:, :, 0:3].rearrange("a g q -> a q g"), row_f[:, :, :]))
            rest(0, 0)
            rest(0, 1)
            dve.wait_ge(s_base_ps, 1)
            meta(nc.vector.tensor_copy(base_bc[:, :], psS[:, 0:NG]))
            dve.wait_ge(s_dwt, 2)
            meta(nc.vector.tensor_tensor(dw_tab[:, :, 0, :], dw_tab[:, :, 0, :],
                                         base_bc[:, :].unsqueeze(2).to_broadcast([P, NG, J]), ALU.subtract))
            nc.vector.memset(dw_tab[0:TWICE // J, LAST, 0, :], -1e6).then_inc(s_tables, 1)

            def onehots(slot, done):
                for j in range(J):
                    last = nc.vector.tensor_scalar(onehot[:, slot % 2, j, :], iota[:, :], dw[:, slot, 0, j:j + 1],
                                                   None, ALU.is_equal)
                last.then_inc(done, 1)

            def first_onehots(layer, b, s, shift):
                dve.wait_ge(s_dw[layer], b * SLOTS + (s + shift + 1))
                onehots((s + shift) % SLOTS, s_oh[layer])

            def width(layer, i):
                return PE3 if layer == 0 and i == 0 else PE2

            def offsets(layer, i, turn, q):
                w = width(layer, i)
                dve.wait_ge(s_bc[layer][i], turn * (32 if w == PE3 else 16))
                nc.vector.tensor_scalar(src_off[:, 0:w], src_bc[:, i, 0:w], node_f[:, 0:1], None,
                                        ALU.subtract).then_inc(s_off[layer], 1)
                dve.wait_ge(s_off[layer], q + 1)

            def pick_half(layer, i, half):
                w = width(layer, i)
                for n in range(half * NK // 2, (half + 1) * NK // 2):
                    last = nc.vector.tensor_scalar(pick[i][0:PN, n, 0:w], src_off[:, 0:w],
                                                   float(n // KN * CHUNK + n % KN), None, ALU.is_equal)
                if half == 1:
                    last.then_inc(s_pick[layer], 1)
                return last

            def next_pick(layer, b, s):
                if s % 2:
                    dve.wait_ge(s_picked[layer], b * SLOTS + (s + 1))
                    dve.wait_ge(s_pick[layer], 2 * b + (s + 3) // 2)
                    if layer == 0 and s == 1:
                        dve.wait_ge(s_xused, b + 1)
                    offsets(layer, (s + 3) // 2 % 2, b + ((s + 3) // 4 + 1), 2 * b + (s + 3) // 2)
                    last = pick_half(layer, (s + 3) // 2 % 2, 0)
                    if layer == 0 and s == 1:
                        last.then_inc(s_half, 1)
                else:
                    pick_half(layer, (s // 2 + 1) % 2, 1)

            def second_pick(layer):
                dve.wait_ge(s_pick[layer], 1)
                offsets(layer, 1, 1, 1)
                pick_half(layer, 1, 0)

            def picked_rows(layer, b, s, shift):
                slot = (s + shift) % SLOTS
                dve.wait_ge(s_picked[layer], b * SLOTS + (s + shift + 1))
                nc.vector.tensor_reduce(rows[:, slot, JG, 0:D], psG[slot % 2].rearrange("p (q d) -> p d q", q=SPLIT),
                                        AX.X, ALU.add).then_inc(s_prow[layer], 1)

            def extra_rows(b):
                dve.wait_ge(s_xpicked, b + 1)
                nc.vector.tensor_reduce(rows[:, EXTRA, JG - 1, 0:D], psX.rearrange("p (q d) -> p d q", q=SPLIT),
                                        AX.X, ALU.add).then_inc(s_xrow, 1)

            def windows_of(b, s):
                g = b * SLOTS + s
                base = dve.value_load(row_i[0:1, bass.ds(g, 1), 0], min_val=0, max_val=N - 1)
                count = dve.value_load(row_i[0:1, bass.ds(g, 1), 1], min_val=1, max_val=MAXW)
                return base, count

            def sums(layer, b, s, width, base, count):
                g = b * SLOTS + s
                par = s % 2
                dve.wait_ge(s_win[layer], b * SLOTS + (s + 1))
                dve.wait_ge(s_acc[layer], b * SLOTS + (s + 2))
                to = sums_sb[0:width, bass.ds(base, WIN)]
                nc.vector.tensor_tensor(to, to, psW[par][0:width, :], ALU.add).then_inc(s_acc[layer], 1)
                with dve.If(count > 1):
                    before = dve.value_load(row_i[0:1, bass.ds(g, 1), 2], min_val=0, max_val=MAXW * NG)
                    dve.wait_ge(s_acc[layer], b * SLOTS + (s + 3))
                    dve.sem_inc(s_passed, 1)
                    with dve.Fori(0, count - 1) as i:
                        k = before + i + 1
                        nc.vector.tensor_scalar_add(dw[:, s, 0, :], dw[:, s, 0, :],
                                                    -float(WIN)).then_inc(s_more_dw[layer], 1)
                        dve.wait_ge(s_more_dw[layer], k)
                        onehots(s, s_more_oh[layer])
                        dve.wait_ge(s_more_win[layer], k)
                        at_node = nc.s_assert_within(base + i * WIN + WIN, 0, N - 1, skip_runtime_bounds_check_because=(
                            "a group has just enough windows to reach its greatest target, which is below N"))
                        to = sums_sb[0:width, bass.ds(at_node, WIN)]
                        nc.vector.tensor_tensor(to, to, psW[par][0:width, :], ALU.add).then_inc(s_more_acc[layer], 1)
                        dve.wait_ge(s_more_acc[layer], k)
                nc.vector.memset(tick[:, s:s + 1], 0.0).then_inc(s_done, 1)

            for u in range(UNITS):
                low(0, u)
                if u + 2 < UNITS:
                    rest(0, u + 2)
            dve.wait_ge(s_tr, 6)
            offsets(0, 0, 1, 0)
            pick_half(0, 0, 0)
            pick_half(0, 0, 1)
            dve.wait_ge(s_zero, 1)
            first_onehots(0, 0, 0, 0)
            second_pick(0)
            picked_rows(0, 0, 0, 0)

            def first(b, last_body):
                for s in range(SLOTS):
                    if not (last_body and s == SLOTS - 1):
                        first_onehots(0, b, s, 1)
                    if not last_body or s == 0:
                        next_pick(0, b, s)
                    base, count = windows_of(b, s)
                    if not (last_body and s == SLOTS - 1):
                        picked_rows(0, b, s, 1)
                        if s == 1:
                            extra_rows(b)
                    if last_body and s == 1:
                        dve.wait_ge(s_picked[0], NG - 2)
                        dve.wait_ge(s_pick[0], PAIRS)
                        offsets(1, 0, 1, 0)
                        pick_half(1, 0, 0)
                    elif last_body and s == 2:
                        pick_half(1, 0, 1)
                    elif last_body and s == 3:
                        dve.wait_ge(s_picked[0], NG)
                        second_pick(1)
                    sums(0, b, s, DA, base, count)

            with dve.Fori(0, BODIES - 1) as b:
                first(b, False)
            first(BODIES - 1, True)

            def residual(u):
                dve.wait_ge(s_agg, u + 1)
                agg = psU[u % 2][0:PN, :, 0:KN * DA].rearrange("p c (k f) -> p c k f", f=DA)
                xu = unit(x_sb, u).rearrange("p c (k d) -> p c k d", d=D)
                hu = unit(h_sb, u).rearrange("p c (k d) -> p c k d", d=D)
                step(nc.vector.tensor_scalar_add(deg[:, 0, :, :], agg[:, :, :, D], DEG_EPS))
                step(nc.vector.reciprocal(deg[:, 1, :, :], deg[:, 0, :, :]))
                step(nc.vector.tensor_tensor(hu, agg[:, :, :, 0:D],
                                             deg[:, 1, :, :].unsqueeze(3).to_broadcast([PN, UC, KN, D]), ALU.mult))
                nc.vector.scalar_tensor_tensor(out=xu, in0=hu, scalar=0.0, in1=xu,
                                               op0=ALU.max, op1=ALU.add).then_inc(s_x1, 1)
                dve.wait_ge(s_x1, u + 1)

            def table_rows(u):
                dve.wait_ge(s_tab, u + 1)
                flat = unit(h_sb, u).rearrange("p c e -> p (c e)")
                for i, (lo, hi) in enumerate(((0, BANK), (BANK, UD))):
                    last = nc.vector.tensor_tensor(
                        flat[:, lo:hi].rearrange("p (t d) -> p t d", d=D),
                        psP[i][0:PN, 0:hi - lo].rearrange("p (t d) -> p t d", d=D),
                        bm_bc[:, :].unsqueeze(1).to_broadcast([PN, (hi - lo) // D, D]), ALU.add)
                last.then_inc(s_tabc, 1)

            dve.wait_ge(s_w, 16 * 10)
            nc.vector.tensor_scalar_add(scale1[:, :], eps_sb[:, :], 1.0).then_inc(s_scale, 1)
            dve.wait_ge(s_scale, 1)
            for u in range(UNITS + 2):
                if u < UNITS:
                    residual(u)
                    centre(1, u)
                if 1 <= u <= UNITS:
                    variance(1, u - 1)
                if 1 <= u <= UNITS:
                    normed(1, u - 1)
                if u >= 2:
                    table_rows(u - 2)
            dve.wait_ge(s_seed, UNITS)
            rest(1, 0)
            for u in range(UNITS):
                if u + 1 < UNITS:
                    rest(1, u + 1)
                low(1, u)

            def message_sum(b, s, shift):
                slot = (s + shift) % SLOTS
                g = b * SLOTS + (s + shift)
                dve.wait_ge(s_em, g + 1)
                dve.wait_ge(s_gat[slot], BODIES * 16 * JP[0][slot] + (b + (s + shift) // SLOTS + 1) * (16 * JG))
                dve.wait_ge(s_prow[1], g + 2)
                dve.wait_ge(s_msg, g + 1)
                nc.vector.tensor_tensor(pre[:, slot % 2, :].rearrange("p (j d) -> p j d", d=D),
                                        psM.rearrange("p (j d) -> p j d", d=D), rows[:, slot, :, 0:D],
                                        ALU.add).then_inc(s_used[slot], 1)

            first_onehots(1, 0, 0, 0)
            picked_rows(1, 0, 0, 0)
            message_sum(0, 0, 0)

            def second(b, last_body):
                for s in range(SLOTS):
                    if not (last_body and s == SLOTS - 1):
                        first_onehots(1, b, s, 1)
                    if not last_body or s == 0:
                        next_pick(1, b, s)
                    base, count = windows_of(b, s)
                    if not (last_body and s == SLOTS - 1):
                        picked_rows(1, b, s, 1)
                        message_sum(b, s, 1)
                    sums(1, b, s, D, base, count)

            with dve.Fori(0, BODIES - 1) as b:
                second(b, False)
            second(BODIES - 1, True)

            for c in range(NC):
                dve.wait_ge(s_fin_g, c + 1)
                nc.vector.tensor_tensor(h_sb[:, c, :], h_sb[:, c, :], x_sb[:, c, :], ALU.add).then_inc(s_fin, 1)


_INS = ["x", "src", "dst", "edge_attr_64", "edge_weight", "L0_gnn_W", "L0_gnn_b", "L1_gnn_W_msg",
        "L1_gnn_b_msg", "L1_gnn_W_upd", "L1_gnn_b_upd", "L1_gnn_eps"]
_OUTS = [((6250, 64), "float32")]


def kernel(**inputs):
    import numpy as _np
    import concourse.bacc as _bacc
    from concourse import mybir as _mybir
    from concourse.bass_utils import run_bass_kernel_spmd as _run

    nc = _bacc.Bacc("TRN2", target_bir_lowering=False, num_devices=1)
    arrays, args = {}, []
    for name in _INS:
        a = _np.ascontiguousarray(inputs[name])
        arrays[f"in_{name}_dram"] = a
        args.append(nc.dram_tensor(f"in_{name}_dram", a.shape, _mybir.dt.from_np(a.dtype), kind="ExternalInput").ap())
    for i, (shape, dtype) in enumerate(_OUTS):
        dt = _mybir.dt.from_np(_np.dtype(dtype))
        args.append(nc.dram_tensor(f"out_{i}_dram", shape, dt, kind="ExternalOutput").ap())
    two_layer_gnn(nc, *args)
    r = _run(nc, [arrays], core_ids=[0])
    got = tuple(r.results[0][f"out_{i}_dram"] for i in range(len(_OUTS)))
    return got[0]
```
